# Optimizing a Trainium2 kernel written in Bass

```python
import numpy as np
import jax
import jax.numpy as jnp

def _softmax(x, axis=-1):
    return jax.nn.softmax(x, axis=axis)

def _gelu(x):
    return jax.nn.gelu(x, approximate=True)

def _silu(x):
    return jax.nn.silu(x)

def _sigmoid(x):
    return jax.nn.sigmoid(x)

def _layernorm(x, axis=-1, eps=1e-05):
    m = jnp.mean(x, axis=axis, keepdims=True)
    v = jnp.var(x, axis=axis, keepdims=True)
    return (x - m) / jnp.sqrt(v + eps)

def _scatter_add(tgt, idx, src, axis=0):
    return tgt.at[idx].add(src)

def _segment_sum(src, seg, n):
    return jax.ops.segment_sum(src, seg, n)
kernel_name = 'mk_prb_d1_jaxref_r8_658770'

def setup_inputs(seed: int=0):
    np.random.seed(seed)
    _w = jnp.asarray

    def _L0_attn_setup():
        import jax, jax.numpy as jnp
        import numpy as np
        import itertools
        B, T, C, H = (2, 256, 128, 8)
        HD = C // H

        def _head_dirs():
            signs = [-1.0, 1.0]
            tri = np.array(list(itertools.product(signs, repeat=3)), dtype=np.float32)
            tri = tri / np.linalg.norm(tri, axis=1, keepdims=True)
            return jnp.asarray(tri[:H])
        key = jax.random.key(seed)
        ks = jax.random.split(key, 5)
        w = lambda k, sh: jax.random.normal(k, sh, dtype=jnp.float32) * 0.02
        return {'x': jax.random.normal(ks[0], (B, T, C), dtype=jnp.float32), 'Wq': w(ks[1], (H * 3, C)), 'Wk': w(ks[2], (H * 3, C)), 'Wv': w(ks[3], (C, C)), 'Wo': w(ks[4], (C, C)), 'scale': jnp.asarray(1.0 / np.sqrt(3.0), dtype=jnp.float32)}
    _L0_attn_in = _L0_attn_setup()

    def _L0_ffn_setup():
        import jax, jax.numpy as jnp
        import numpy as np

        def _bitlinear(x, w_latent):
            scale = jax.lax.stop_gradient(jnp.clip(jnp.mean(jnp.abs(w_latent), axis=1, keepdims=True), 1e-05, None))
            tern = jnp.clip(jnp.round(w_latent / scale), -1.0, 1.0)
            w = w_latent + jax.lax.stop_gradient(tern - w_latent)
            return x @ (w * scale).T
        key = jax.random.key(seed)
        ks = jax.random.split(key, 6)
        dim, hidden, rank = (128, 512, 16)
        B, S = (4, 512)
        x = jax.random.normal(ks[0], (B, S, dim), dtype=jnp.float32)
        w_fc = 0.02 * jax.random.normal(ks[1], (hidden, dim), dtype=jnp.float32)
        w_proj = 0.02 * jax.random.normal(ks[2], (dim, hidden), dtype=jnp.float32)
        u = 0.02 * jax.random.normal(ks[3], (hidden, rank), dtype=jnp.float32)
        v = 0.02 * jax.random.normal(ks[4], (rank, dim), dtype=jnp.float32)
        fast_b = jax.random.normal(ks[5], (rank, rank), dtype=jnp.float32)
        gate = jnp.float32(0.05)
        return {'x': x, 'fast_b': fast_b, 'w_fc': w_fc, 'w_proj': w_proj, 'u': u, 'v': v, 'gate': gate}
    _L0_ffn_in = _L0_ffn_setup()
    _d = {'L0_attn_x': _L0_attn_in['x'], 'L0_attn_Wq': _L0_attn_in['Wq'], 'L0_attn_Wk': _L0_attn_in['Wk'], 'L0_attn_Wv': _L0_attn_in['Wv'], 'L0_attn_Wo': _L0_attn_in['Wo'], 'L0_attn_scale': _L0_attn_in['scale'], 'L0_ffn_fast_b': _L0_ffn_in['fast_b'], 'L0_ffn_w_fc': _L0_ffn_in['w_fc'], 'L0_ffn_w_proj': _L0_ffn_in['w_proj'], 'L0_ffn_u': _L0_ffn_in['u'], 'L0_ffn_v': _L0_ffn_in['v'], 'L0_ffn_gate': _L0_ffn_in['gate']}
    _x0 = _d['L0_attn_x']
    _d['L0_attn_x'] = jax.random.normal(jax.random.fold_in(jax.random.key(seed), 1), (2, 1024, 128), dtype=_x0.dtype)
    del _x0
    return _d

def reference(L0_attn_x, L0_attn_Wq, L0_attn_Wk, L0_attn_Wv, L0_attn_Wo, L0_attn_scale, L0_ffn_fast_b, L0_ffn_w_fc, L0_ffn_w_proj, L0_ffn_u, L0_ffn_v, L0_ffn_gate):

    def _L0_attn_ref(x, Wq, Wk, Wv, Wo, scale):
        import jax, jax.numpy as jnp
        import numpy as np
        import itertools
        B, T, C, H = (2, 256, 128, 8)
        HD = C // H

        def _head_dirs():
            signs = [-1.0, 1.0]
            tri = np.array(list(itertools.product(signs, repeat=3)), dtype=np.float32)
            tri = tri / np.linalg.norm(tri, axis=1, keepdims=True)
            return jnp.asarray(tri[:H])
        Bb, Tt, Cc = x.shape
        dirs = _head_dirs()
        q3 = (x @ Wq.T).reshape(Bb, Tt, H, 3).transpose(0, 2, 1, 3)
        k3 = (x @ Wk.T).reshape(Bb, Tt, H, 3).transpose(0, 2, 1, 3)
        v = (x @ Wv.T).reshape(Bb, Tt, H, HD).transpose(0, 2, 1, 3)
        q_on_dir = jnp.einsum('bhtd,hd->bht', q3, dirs)
        k_on_dir = jnp.einsum('bhtd,hd->bht', k3, dirs)
        scores = jnp.einsum('bhtd,bhsd->bhts', q3, k3) * scale + q_on_dir[..., :, None] * k_on_dir[..., None, :]
        causal = jnp.tril(jnp.ones((Tt, Tt), dtype=bool))
        scores = jnp.where(causal, scores, -jnp.inf)
        attn = jax.nn.softmax(scores, axis=-1)
        out = jnp.einsum('bhts,bhsd->bhtd', attn, v)
        out = out.transpose(0, 2, 1, 3).reshape(Bb, Tt, Cc)
        return out @ Wo.T

    def _L0_ffn_ref(x, fast_b, w_fc, w_proj, u, v, gate):
        import jax, jax.numpy as jnp
        import numpy as np

        def _bitlinear(x, w_latent):
            scale = jax.lax.stop_gradient(jnp.clip(jnp.mean(jnp.abs(w_latent), axis=1, keepdims=True), 1e-05, None))
            tern = jnp.clip(jnp.round(w_latent / scale), -1.0, 1.0)
            w = w_latent + jax.lax.stop_gradient(tern - w_latent)
            return x @ (w * scale).T
        h = _bitlinear(x, w_fc) + gate * (x @ v.T @ fast_b.T @ u.T)
        r = jnp.maximum(h, 0.0)
        return _bitlinear(r * r, w_proj)
    x = L0_attn_x
    xn = _layernorm(x, axis=-1)
    x = x + _L0_attn_ref(xn, L0_attn_Wq, L0_attn_Wk, L0_attn_Wv, L0_attn_Wo, L0_attn_scale) + _L0_ffn_ref(xn, L0_ffn_fast_b, L0_ffn_w_fc, L0_ffn_w_proj, L0_ffn_u, L0_ffn_v, L0_ffn_gate)
    return x

_drawn_inputs = setup_inputs


def setup_inputs(seed=0):
    import zlib

    import numpy as np

    out = dict(_drawn_inputs(seed))
    spreads = {}
    factors = {'L0_attn_Wq': 8.0,
     'L0_attn_Wk': 8.0,
     'L0_attn_Wv': 8.0,
     'L0_attn_Wo': 8.0,
     'L0_ffn_fast_b': 8.0,
     'L0_ffn_w_fc': 4.266,
     'L0_ffn_w_proj': 3.242,
     'L0_ffn_u': 8.0,
     'L0_ffn_v': 8.0}
    for name, (base, spread) in spreads.items():
        noise = np.random.default_rng([zlib.crc32(name.encode()), seed]).standard_normal(out[name].shape)
        drawn = base * np.exp(spread * noise) if base else spread * noise
        out[name] = jnp.asarray(drawn.astype(out[name].dtype))
    for name, factor in factors.items():
        out[name] = (out[name] * factor).astype(out[name].dtype)
    return out
```

```python
import concourse.bass as bass
from concourse import mybir
from contextlib import ExitStack
import numpy as np

B, T, C, H = 2, 1024, 128, 8
HD = C // H
HID, RANK = 512, 16
P = 128
NT = B * T // P
TPB = T // P
HG = 4
G = H // HG
CH = 512
NCH = T // CH
TPC = CH // P
NC = B * G * NCH
HC = HID // P
NPART = 3
NQ = 3 * H
MROW = 3 * NPART * NPART
NEG = -1.0e30
LN_EPS = 1e-05
MIN_SCALE = 1e-05
PSLOTS = 4

CID, CMASK, CSEL = 0, P, 2 * P
CDIR = CSEL + 8 * P
CONE = CDIR + NQ
CEND = CONE + 1


def constants():
    k = np.zeros((P, CEND), np.float32)
    k[:, CID:CID + P] = np.eye(P)
    k[:, CMASK:CMASK + P] = np.where(np.arange(P)[None, :] > np.arange(P)[:, None], NEG, 0.0)
    for g in range(G):
        for j in range(HG):
            for i in range(NPART):
                for n in range(NPART):
                    for d in range(3):
                        col = 32 * j + 3 * (NPART * i + n) + d
                        comp = 3 * (HG * g + j) + d
                        for side, part, row in ((0, i, comp), (1, n, NQ + comp)):
                            low = part == 2
                            at = CSEL + ((2 * side + low) * G + g) * P + col
                            k[row if low else row + 64 * part, at] = 1.0
    signs = np.array([[-1.0 if not (h >> (2 - d)) & 1 else 1.0 for d in range(3)] for h in range(H)], np.float32)
    dirs = signs / np.linalg.norm(signs, axis=1, keepdims=True)
    for h in range(H):
        k[3 * h:3 * h + 3, CDIR + 3 * h:CDIR + 3 * h + 3] = np.outer(dirs[h], dirs[h])
    for j in range(HG):
        k[32 * j + MROW:32 * j + MROW + NPART, CONE] = 1.0
    return k


def coords(c):
    return c // (G * NCH), c // NCH % G, c % NCH


def max_units(c):
    chunk = coords(c)[2]
    units = []
    for i in range(TPC * chunk, TPC * (chunk + 1)):
        for half in range(chunk + 1):
            keys = min(CH, P * (i + 1) - CH * half)
            units += [(i, half, h, keys) for h in range(HG)]
    return units


def steps(c):
    chunk = coords(c)[2]
    out = []
    for j in range(TPC * (chunk + 1)):
        first = max(0, P * (j - TPC * chunk))
        out.append((j, first, CH - first))
    return out


STEP0 = [sum(len(steps(k)) for k in range(c)) for c in range(NC + 1)]


def schedule():
    vec, act = [], []
    for c in range(NC):
        vec += [("max", c, u) for u in range(len(max_units(c)))]
        vec.append(("prep", c, 0))
    merged = []
    for item in vec:
        merged.append(item)
    vec = []
    held = None
    since = 0
    for item in merged:
        if item[0] == "prep":
            vec.append(item)
            held, since = ("maxT", item[1], 0), 0
            continue
        vec.append(item)
        if held:
            since += 1
            if since == 3:
                vec.append(held)
                held = None
    if held:
        vec.append(held)
    act = [("ffn", f, 0) for f in range(B * HC)]
    last = None
    for c in range(NC):
        for n in range(len(steps(c))):
            act += [("st", c, n, 0), ("st", c, n, 1)]
            if last:
                act.append(("pv",) + last)
                if last[1] == len(steps(last[0])) - 1:
                    act.append(("norm", last[0]))
            last = (c, n)
    act += [("pv",) + last, ("norm", last[0])]
    order, tv, ta, ready = [], 0.0, 0.0, {}
    vec, act = list(vec), list(act)
    late = []
    while vec or act:
        item = act[0] if act else None
        free = item is not None and (item[0] != "st" or item[1] in ready)
        if item is not None and item[0] == "st" and free:
            ta = max(ta, ready[item[1]])
        if free and (not vec or ta <= tv):
            act.pop(0)
            order.append(item)
            if item[0] == "st":
                ta += 72 + 0.833 * 2 * steps(item[1])[item[2]][2]
            elif item[0] == "ffn":
                ta += 1700
            elif item[0] == "norm":
                tv += 1900
                b, g, chunk = coords(item[1])
                if g == G - 1:
                    late.append([6, ("y", b, chunk)])
        else:
            item = vec.pop(0)
            order.append(item)
            if item[0] == "max":
                u = max_units(item[1])[item[2]]
                tv += 67 + 1.04 * u[3]
            elif item[0] == "maxT":
                tv += 600
                ready[item[1]] = tv + 500
        for x in late:
            x[0] -= 1
        while late and late[0][0] <= 0:
            order.append(late.pop(0)[1])
    order += [x[1] for x in late]
    return order


ORDER = schedule()
VEC_PREP = ["wqk", "wvo", "lora_u", "lora_b", "w1", "w2"]
ACT_PREP = [(kind, b) for b in range(B) for kind in ("xT", "qk", "sel0", "sel1", "sel2", "sel3", "v")]
VEC_UNITS = VEC_PREP + [x for x in ORDER if x[0] in ("max", "maxT", "y")]
ACT_UNITS = ACT_PREP + [x for x in ORDER if x[0] in ("ffn", "st")]
VEC_AT = {x: n for n, x in enumerate(VEC_UNITS)}
ACT_AT = {x: n for n, x in enumerate(ACT_UNITS)}


def build(nc, x, Wq, Wk, Wv, Wo, scale, fast_b, w_fc, w_proj, u, v, gate, consts, out):
    f32, bf16 = mybir.dt.float32, mybir.dt.bfloat16
    ALU, ACT, AX = mybir.AluOpType, mybir.ActivationFunctionType, mybir.AxisListType
    ctx = ExitStack()
    with ctx:
        def sb(name, shape, dt=f32):
            return ctx.enter_context(nc.sbuf_tensor(name, shape, dt))

        def ps(name, shape):
            return ctx.enter_context(nc.psum_tensor(name, shape, f32))

        def sem(name):
            return ctx.enter_context(nc.semaphore(name))

        x_sb = sb("x_sb", [P, NT, C])
        xn = sb("xn", [P, NT, C])
        xnT = sb("xnT", [P, B * T])
        k_sb = sb("k_sb", [P, CEND])
        ident = k_sb[:, CID:CID + P]
        ident16 = sb("ident16", [P, P], bf16)
        mask16 = sb("mask16", [P, P], bf16)
        sel16 = sb("sel16", [P, 8, P], bf16)
        Wq_sb, Wk_sb = sb("Wq_sb", [NQ, C]), sb("Wk_sb", [NQ, C])
        Wv_sb, Wo_sb = sb("Wv_sb", [P, C]), sb("Wo_sb", [P, C])
        Wo_pad = sb("Wo_pad", [P, G, HG, 32])
        scale_c, gate_c = sb("scale_c", [NQ, 1]), sb("gate_c", [RANK, 1])
        mix = sb("mix", [NQ, NQ])
        wqkT = sb("wqkT", [P, 2 * NQ])
        wvoT = sb("wvoT", [P, 3, P])
        wfc_sb, wpj_sb = sb("wfc_sb", [P, HC, C]), sb("wpj_sb", [P, HID])
        u_sb, v_sb = sb("u_sb", [P, HC, RANK]), sb("v_sb", [RANK, C])
        fb_sb = sb("fb_sb", [RANK, RANK])
        loraB, uT = sb("loraB", [RANK, HID]), sb("uT", [RANK, HID])
        fc_sc, pj_sc = sb("fc_sc", [P, 3, HC]), sb("pj_sc", [P, 3])
        tern = sb("tern", [P, 2, 2, HC, C])
        w1T, w2T = sb("w1T", [P, HID]), sb("w2T", [P, HC, C])
        stats, mv = sb("stats", [P, NT, 6]), sb("mv", [P, NT, 2])
        var, std, rstd, nwt = sb("var", [P, NT]), sb("std", [P, NT]), sb("rstd", [P, NT]), sb("nwt", [P, NT])
        qk32, res = sb("qk32", [2 * NQ, B * T]), sb("res", [2 * NQ, B * T])
        part_hm, part_lo = sb("part_hm", [P, B * T], bf16), sb("part_lo", [2 * NQ, B * T], bf16)
        Qr, Kr = sb("Qr", [P, G, B * T], bf16), sb("Kr", [P, G, B * T], bf16)
        V = sb("V", [P, NT, H, 32])
        r2 = sb("r2", [P, HC, B * T])
        pm = sb("pm", [P, 2, 2, TPC, HG])
        nmax, nres = sb("nmax", [P, 2, TPC, HG]), sb("nres", [P, TPC, HG])
        M16 = sb("M16", [P, 2, TPC, HG, 32], bf16)
        Pr = sb("Pr", [P, PSLOTS, HG, CH])
        rows, inv = sb("rows", [P, CH]), sb("inv", [P, CH])
        on = sb("on", [P, G, B * T])
        y_sb = xn

        vbank = [ps(f"vbank{i}", [P, CH]) for i in range(2)]
        abank = [ps(f"abank{i}", [P, 2, CH]) for i in range(2)]
        obank = [ps(f"obank{i}", [P, CH]) for i in range(2)]

        ld_x = [sem(f"ld_x{i}") for i in range(4)]
        ld_id, ld_k, ld_qk, ld_vo, ld_fc, ld_pj, ld_lora = (
            sem(n) for n in ("ld_id", "ld_k", "ld_qk", "ld_vo", "ld_fc", "ld_pj", "ld_lora"))
        v_full, v_free, a_full, a_free = (sem(n) for n in ("v_full", "v_free", "a_full", "a_free"))
        dve_chain, pool_chain = sem("dve_chain"), sem("pool_chain")
        mix_ready, wopad_ready, casts_ready, zeros_ready = (
            sem(n) for n in ("mix_ready", "wopad_ready", "casts_ready", "zeros_ready"))
        var_ready, std_ready, xn_ready = sem("var_ready"), sem("std_ready"), sem("xn_ready")
        hi_ready, res_ready, mid_ready, lo_ready = (
            sem(n) for n in ("hi_ready", "res_ready", "mid_ready", "lo_ready"))
        fc_signs, pj_signs, w1_ready, w2_ready = (sem(n) for n in ("fc_signs", "pj_signs", "w1_ready", "w2_ready"))
        r2_ready, maxima_ready, prep_ready, pv_done, norm_done, stored = (
            sem(n) for n in ("r2_ready", "maxima_ready", "prep_ready", "pv_done", "norm_done", "stored"))

        block = ctx.enter_context(nc.Block())

        @block.sync
        def _(sp):
            xv = x.rearrange("b (n p) c -> p (b n) c", p=P)
            q = NT // 4
            sp.dma_start(k_sb[:, CID:CID + P], consts[:, CID:CID + P]).then_inc(ld_id, 16)
            for i in range(4):
                sp.dma_start(x_sb[:, q * i:q * (i + 1), :], xv[:, q * i:q * (i + 1), :]).then_inc(ld_x[i], 16)
            sp.dma_start(k_sb[:, P:CEND], consts[:, P:CEND]).then_inc(ld_k, 16)
            sp.dma_start(wfc_sb[:, :, :], w_fc.rearrange("(j p) c -> p j c", p=P)).then_inc(ld_fc, 16)
            sp.dma_start(wpj_sb[:, :], w_proj).then_inc(ld_pj, 16)
            n = 0
            for item in ORDER:
                if item[0] == "y":
                    _, b, chunk = item
                    sp.wait_ge(v_free, VEC_AT[item] + 1)
                    t0 = b * TPB + chunk * TPC
                    ov = out.rearrange("b (n p) c -> p (b n) c", p=P)
                    sp.dma_start(ov[:, t0:t0 + TPC, :], y_sb[:, t0:t0 + TPC, :]).then_inc(stored, 16)
                    n += 1
            sp.wait_ge(stored, 16 * n)

        @block.gpsimd
        def _(pool):
            chain = [0]

            def link(ins):
                chain[0] += 1
                ins.then_inc(pool_chain, 1)
                pool.wait_ge(pool_chain, chain[0])

            pool.dma_start(Wq_sb[:, :], Wq).then_inc(ld_qk, 16)
            pool.dma_start(Wk_sb[:, :], Wk).then_inc(ld_qk, 16)
            pool.dma_start(scale_c[:, :], scale.to_broadcast([NQ, 1])).then_inc(ld_qk, 16)
            pool.dma_start(Wv_sb[:, :], Wv).then_inc(ld_vo, 16)
            pool.dma_start(Wo_sb[:, :], Wo).then_inc(ld_vo, 16)
            pool.dma_start(u_sb[:, :, :], u.rearrange("(j p) r -> p j r", p=P)).then_inc(ld_lora, 16)
            pool.dma_start(v_sb[:, :], v).then_inc(ld_lora, 16)
            pool.dma_start(fb_sb[:, :], fast_b).then_inc(ld_lora, 16)
            pool.dma_start(gate_c[:, :], gate.to_broadcast([RANK, 1])).then_inc(ld_lora, 16)
            nc.gpsimd.memset(part_hm[:, :], 0.0).then_inc(zeros_ready, 1)
            link(nc.gpsimd.memset(Wo_pad[:, :, :, :], 0.0))
            pool.wait_ge(ld_vo, 32)
            nc.gpsimd.tensor_copy(Wo_pad[:, :, :, 0:HD],
                                  Wo_sb[:, :].rearrange("p (g j d) -> p g j d", g=G, j=HG)).then_inc(wopad_ready, 1)
            nc.gpsimd.memset(V[:, :, :, HD:32], 1.0).then_inc(zeros_ready, 1)
            nc.gpsimd.memset(M16[:, :, :, :, :], 0.0).then_inc(zeros_ready, 1)
            pool.wait_ge(zeros_ready, 3)

            wp = wpj_sb[:, :].rearrange("p (j c) -> p j c", j=HC)
            for k, (w, sc, signs, ready) in enumerate((
                    (wfc_sb[:, :, :], fc_sc[:, 0, :, None].to_broadcast([P, HC, C]), fc_signs, w1_ready),
                    (wp, pj_sc[:, 0:1, None].to_broadcast([P, HC, C]), pj_signs, w2_ready))):
                pool.wait_ge(signs, 2)
                above, below = tern[:, k, 0, :, :], tern[:, k, 1, :, :]
                link(nc.gpsimd.tensor_tensor(above, above, below, ALU.subtract))
                link(nc.gpsimd.tensor_tensor(below, above, w, ALU.subtract))
                link(nc.gpsimd.tensor_tensor(below, below, w, ALU.add))
                nc.gpsimd.tensor_tensor(w, below, sc, ALU.mult).then_inc(ready, 1)

            for item in ORDER:
                if item[0] == "ffn":
                    f = item[1]
                    b, j = f // HC, f % HC
                    r = r2[:, j, b * T:(b + 1) * T]
                    pool.wait_ge(a_free, ACT_AT[item] + 1)
                    nc.gpsimd.tensor_tensor(r, r, r, ALU.mult).then_inc(r2_ready, 1)
                elif item[0] == "prep":
                    c = item[1]
                    s = c % 2
                    pool.wait_ge(maxima_ready, c + 1)
                    if c >= 2:
                        pool.wait_ge(v_full, VEC_AT[("maxT", c - 2, 0)] + 1)
                    neg = nmax[:, s, :, :]
                    m = [M16[:, s, :, :, MROW + k] for k in range(NPART)]
                    link(nc.gpsimd.tensor_copy(m[0], neg))
                    link(nc.gpsimd.tensor_tensor(nres[:, :, :], neg, m[0], ALU.subtract))
                    link(nc.gpsimd.tensor_copy(m[1], nres[:, :, :]))
                    nc.gpsimd.tensor_tensor(m[2], nres[:, :, :], m[1], ALU.subtract).then_inc(prep_ready, 1)
                    pool.wait_ge(prep_ready, c + 1)

        @block.vector
        def _(dve):
            chain = [0]

            def link(ins):
                chain[0] += 1
                ins.then_inc(dve_chain, 1)
                dve.wait_ge(dve_chain, chain[0])

            def full(unit):
                dve.wait_ge(v_full, VEC_AT[unit] + 1)

            dve.wait_ge(ld_qk, 48)
            dve.wait_ge(ld_id, 16)
            dve.wait_ge(ld_k, 16)
            nc.vector.scalar_tensor_tensor(out=mix[:, :], in0=k_sb[0:NQ, CID:CID + NQ], scalar=scale_c[:, 0:1],
                                           in1=k_sb[0:NQ, CDIR:CDIR + NQ], op0=ALU.mult,
                                           op1=ALU.add).then_inc(mix_ready, 1)
            nc.vector.tensor_copy(ident16[:, :], k_sb[:, CID:CID + P]).then_inc(casts_ready, 1)
            nc.vector.tensor_copy(mask16[:, :], k_sb[:, CMASK:CMASK + P]).then_inc(casts_ready, 1)
            nc.vector.tensor_copy(sel16[:, :, :], k_sb[:, CSEL:CDIR].rearrange("p (s c) -> p s c", c=P)
                                  ).then_inc(casts_ready, 1)

            def variances(b):
                t0 = b * TPB
                for n in range(t0, t0 + TPB):
                    if n % 4 == 0:
                        dve.wait_ge(ld_x[n // 4], 16)
                    last = nc.vector.bn_stats(stats[:, n, :], x_sb[:, n, :])
                link(last)
                for n in range(t0, t0 + TPB):
                    last = nc.vector.bn_aggr(mv[:, n, :], stats[:, n, :])
                link(last)
                nc.vector.tensor_scalar(var[:, t0:t0 + TPB], mv[:, t0:t0 + TPB, 1], LN_EPS, None,
                                        ALU.add).then_inc(var_ready, 1)

            def normalise(b):
                t0 = b * TPB
                s = slice(t0, t0 + TPB)
                dve.wait_ge(std_ready, b + 1)
                link(nc.vector.reciprocal(rstd[:, s], std[:, s]))
                link(nc.vector.tensor_tensor(nwt[:, s], rstd[:, s], rstd[:, s], ALU.mult))
                link(nc.vector.tensor_tensor(nwt[:, s], nwt[:, s], var[:, s], ALU.mult))
                link(nc.vector.tensor_scalar(nwt[:, s], nwt[:, s], -0.5, 1.5, ALU.mult, ALU.add))
                link(nc.vector.tensor_tensor(rstd[:, s], rstd[:, s], nwt[:, s], ALU.mult))
                for n in range(t0, t0 + TPB):
                    last = nc.vector.tensor_scalar(xn[:, n, :], x_sb[:, n, :], mv[:, n, 0:1], rstd[:, n:n + 1],
                                                   ALU.subtract, ALU.mult)
                last.then_inc(xn_ready, 1)

            def subtract_first(b):
                cols = slice(b * T, (b + 1) * T)
                dve.wait_ge(hi_ready, b + 1)
                dve.wait_ge(a_free, ACT_AT[("qk", b)] + 1)
                nc.vector.tensor_tensor(res[:, cols], qk32[:, cols], part_hm[0:2 * NQ, cols],
                                        ALU.subtract).then_inc(res_ready, 1)

            def last_parts(b):
                cols = slice(b * T, (b + 1) * T)
                dve.wait_ge(mid_ready, b + 1)
                nc.vector.tensor_tensor(part_lo[:, cols], res[:, cols], part_hm[64:64 + 2 * NQ, cols],
                                        ALU.subtract).then_inc(lo_ready, 1)

            variances(0)
            normalise(0)
            full("wqk")
            nc.vector.tensor_copy(wqkT[:, :], vbank[0][:, 0:2 * NQ]).then_inc(v_free, 1)
            full("wvo")
            nc.vector.tensor_copy(wvoT[:, :, :], vbank[1][:, 0:3 * P].rearrange("p (k c) -> p k c", c=P)
                                  ).then_inc(v_free, 1)
            variances(1)
            subtract_first(0)
            last_parts(0)
            normalise(1)
            dve.wait_ge(ld_fc, 16)
            link(nc.vector.tensor_reduce(out=fc_sc[:, 1, :], in_=wfc_sb[:, :, :], op=ALU.add, axis=AX.X,
                                         apply_absolute_value=True))
            link(nc.vector.tensor_scalar(fc_sc[:, 0, :], fc_sc[:, 1, :], 1.0 / C, MIN_SCALE,
                                         ALU.mult, ALU.max))
            nc.vector.tensor_scalar(fc_sc[:, 1, :], fc_sc[:, 0, :], 0.5, None, ALU.mult)
            link(nc.vector.tensor_scalar(fc_sc[:, 2, :], fc_sc[:, 0, :], -0.5, None, ALU.mult))
            for k, op in enumerate((ALU.is_gt, ALU.is_lt)):
                nc.vector.tensor_tensor(tern[:, 0, k, :, :], wfc_sb[:, :, :],
                                        fc_sc[:, 1 + k, :, None].to_broadcast([P, HC, C]),
                                        op).then_inc(fc_signs, 1)
            dve.wait_ge(ld_pj, 16)
            link(nc.vector.tensor_reduce(out=pj_sc[:, 1:2], in_=wpj_sb[:, :], op=ALU.add, axis=AX.X,
                                         apply_absolute_value=True))
            link(nc.vector.tensor_scalar(pj_sc[:, 0:1], pj_sc[:, 1:2], 1.0 / HID, MIN_SCALE,
                                         ALU.mult, ALU.max))
            nc.vector.tensor_scalar(pj_sc[:, 1:2], pj_sc[:, 0:1], 0.5, None, ALU.mult)
            link(nc.vector.tensor_scalar(pj_sc[:, 2:3], pj_sc[:, 0:1], -0.5, None, ALU.mult))
            for k, op in enumerate((ALU.is_gt, ALU.is_lt)):
                nc.vector.tensor_scalar(tern[:, 1, k, :, :].rearrange("p j c -> p (j c)"), wpj_sb[:, :],
                                        pj_sc[:, 1 + k:2 + k], None, op).then_inc(pj_signs, 1)
            subtract_first(1)
            last_parts(1)
            full("lora_u")
            nc.vector.tensor_copy(uT[:, :], vbank[0][0:RANK, :]).then_inc(v_free, 1)
            full("lora_b")
            nc.vector.tensor_scalar(loraB[:, :], vbank[1][0:RANK, :], gate_c[:, 0:1], None,
                                    ALU.mult).then_inc(v_free, 1)
            full("w1")
            nc.vector.tensor_copy(w1T[:, :], vbank[0][:, :]).then_inc(v_free, 1)
            full("w2")
            nc.vector.tensor_copy(w2T[:, :, :], vbank[1][:, :].rearrange("p (j c) -> p j c", j=HC)
                                  ).then_inc(v_free, 1)

            for item in ORDER:
                kind = item[0]
                if kind == "max":
                    c = item[1]
                    i, half, h, keys = max_units(c)[item[2]]
                    if item[2] == 0 and c >= 2:
                        dve.wait_ge(prep_ready, c - 1)
                    full(item)
                    nc.vector.tensor_reduce(out=pm[:, c % 2, half, i % TPC, h:h + 1],
                                            in_=vbank[VEC_AT[item] % 2][:, 0:keys], op=ALU.max, axis=AX.X,
                                            negate=True).then_inc(v_free, 1)
                elif kind == "prep":
                    c = item[1]
                    dve.wait_ge(v_free, VEC_AT[("max", c, len(max_units(c)) - 1)] + 1)
                    nc.vector.tensor_tensor(nmax[:, c % 2, :, :], pm[:, c % 2, 0, :, :],
                                            pm[:, c % 2, coords(c)[2], :, :], ALU.min).then_inc(maxima_ready, 1)
                elif kind == "maxT":
                    c = item[1]
                    b, g, chunk = coords(c)
                    q = Qr[:, g, b * T + chunk * CH:b * T + (chunk + 1) * CH]
                    full(item)
                    nc.vector.tensor_tensor(q, vbank[VEC_AT[item] % 2][:, :], q, ALU.add).then_inc(v_free, 1)
                elif kind == "norm":
                    c = item[1]
                    b, g, chunk = coords(c)
                    o = obank[c % 2]
                    dve.wait_ge(pv_done, STEP0[c + 1])
                    link(nc.vector.stream_shuffle(rows[:, :], o[:, :], [HD + k % HD for k in range(32)]))
                    link(nc.vector.reciprocal(inv[:, :], rows[:, :]))
                    nc.vector.tensor_tensor(on[:, g, b * T + chunk * CH:b * T + (chunk + 1) * CH], o[:, :],
                                            inv[:, :], ALU.mult).then_inc(norm_done, 1)
                    dve.wait_ge(norm_done, c + 1)
                elif kind == "y":
                    _, b, chunk = item
                    t0 = b * TPB + chunk * TPC
                    full(item)
                    src = vbank[VEC_AT[item] % 2][:, :].rearrange("p (n c) -> p n c", n=TPC)
                    nc.vector.tensor_tensor(y_sb[:, t0:t0 + TPC, :], src, x_sb[:, t0:t0 + TPC, :],
                                            ALU.add).then_inc(v_free, 1)

        @block.scalar
        def _(act):
            def full(unit):
                act.wait_ge(a_full, ACT_AT[unit] + 1)

            def deviations(b):
                act.wait_ge(var_ready, b + 1)
                nc.scalar.activation(std[:, b * TPB:(b + 1) * TPB], var[:, b * TPB:(b + 1) * TPB],
                                     ACT.Sqrt).then_inc(std_ready, 1)

            deviations(0)
            for b in range(B):
                cols = slice(b * T, (b + 1) * T)

                def bank(unit):
                    return abank[ACT_AT[unit] % 2]

                full(("xT", b))
                nc.scalar.copy(xnT[:, cols], bank(("xT", b))[:, :, :].rearrange("p a n -> p (a n)")
                               ).then_inc(a_free, 1)
                full(("qk", b))
                src = bank(("qk", b))[0:2 * NQ, :, :].rearrange("p a n -> p (a n)")
                if b == 0:
                    act.wait_ge(zeros_ready, 3)
                nc.scalar.copy(part_hm[0:2 * NQ, cols], src).then_inc(hi_ready, 1)
                nc.scalar.copy(qk32[:, cols], src).then_inc(a_free, 1)
                if b == 0:
                    deviations(1)
                act.wait_ge(res_ready, b + 1)
                nc.scalar.copy(part_hm[64:64 + 2 * NQ, cols], res[:, cols]).then_inc(mid_ready, 1)
                for s in range(4):
                    g = s // 2
                    unit = (f"sel{s}", b)
                    full(unit)
                    src = bank(unit)[:, :, :].rearrange("p a n -> p (a n)")
                    if s % 2 == 0:
                        nc.scalar.copy(Qr[:, g, cols], src).then_inc(a_free, 1)
                    else:
                        nc.scalar.activation(Kr[:, g, cols], src, ACT.Identity,
                                             bias=k_sb[:, CONE:CONE + 1]).then_inc(a_free, 1)
                full(("v", b))
                nc.scalar.copy(V[:, b * TPB:(b + 1) * TPB, :, 0:HD],
                               bank(("v", b))[:, :, :].rearrange("p a (n h d) -> p (a n) h d", h=H, d=HD)
                               ).then_inc(a_free, 1)

            for item in ORDER:
                if item[0] == "ffn":
                    b, j = item[1] // HC, item[1] % HC
                    full(item)
                    nc.scalar.activation(r2[:, j, b * T:(b + 1) * T],
                                         abank[ACT_AT[item] % 2][:, :, :].rearrange("p a n -> p (a n)"),
                                         ACT.Relu).then_inc(a_free, 1)
                elif item[0] == "st":
                    _, c, step, pair = item
                    n = STEP0[c] + step
                    cols = steps(c)[step][2]
                    if n >= PSLOTS and pair == 0:
                        act.wait_ge(pv_done, n - PSLOTS + 1)
                    full(item)
                    nc.scalar.activation(Pr[:, n % PSLOTS, 2 * pair:2 * pair + 2, 0:cols],
                                         abank[ACT_AT[item] % 2][:, :, 0:cols], ACT.Exp).then_inc(a_free, 1)

        @block.tensor
        def _(pe):
            def vb(unit):
                n = VEC_AT[unit]
                if n >= 2:
                    pe.wait_ge(v_free, n - 1)
                return vbank[n % 2]

            def ab(unit):
                n = ACT_AT[unit]
                if n >= 2:
                    pe.wait_ge(a_free, n - 1)
                return abank[n % 2]

            pe.wait_ge(ld_qk, 48)
            pe.wait_ge(ld_id, 16)
            pe.wait_ge(mix_ready, 1)
            o = vb("wqk")
            nc.tensor.matmul(o[:, 0:NQ], Wq_sb[:, :], mix[:, :], start=True, stop=True)
            nc.tensor.matmul(o[:, NQ:2 * NQ], Wk_sb[:, :], k_sb[0:NQ, CID:CID + NQ], start=True,
                             stop=True).then_inc(v_full, 1)
            pe.wait_ge(ld_vo, 32)
            pe.wait_ge(wopad_ready, 1)
            o = vb("wvo")
            nc.tensor.transpose(o[:, 0:P], Wv_sb[:, :], ident)
            for g in range(G):
                last = nc.tensor.transpose(o[:, (g + 1) * P:(g + 2) * P],
                                           Wo_pad[:, g, :, :].rearrange("p j d -> p (j d)"), ident)
            last.then_inc(v_full, 1)

            for b in range(B):
                t0 = b * TPB
                pe.wait_ge(xn_ready, b + 1)
                o = ab(("xT", b))
                for n in range(TPB):
                    last = nc.tensor.transpose(o[:, n // 4, (n % 4) * P:(n % 4 + 1) * P], xn[:, t0 + n, :], ident)
                last.then_inc(a_full, 1)
                pe.wait_ge(a_free, ACT_AT[("xT", b)] + 1)
                pe.wait_ge(v_free, VEC_AT["wqk"] + 1)
                o = ab(("qk", b))
                for k in range(2):
                    last = nc.tensor.matmul(o[0:2 * NQ, k, :], wqkT[:, :],
                                            xnT[:, b * T + k * CH:b * T + (k + 1) * CH], start=True, stop=True)
                last.then_inc(a_full, 1)
                pe.wait_ge(casts_ready, 3)
                pe.wait_ge(mid_ready, b + 1)
                pe.wait_ge(lo_ready, b + 1)
                for s in range(4):
                    g, side = s // 2, s % 2
                    o = ab((f"sel{s}", b))
                    for k in range(2):
                        cols = slice(b * T + k * CH, b * T + (k + 1) * CH)
                        nc.tensor.matmul(o[:, k, :], sel16[:, 2 * side * G + g, :], part_hm[:, cols],
                                         start=True, stop=False)
                        last = nc.tensor.matmul(o[:, k, :], sel16[0:2 * NQ, (2 * side + 1) * G + g, :],
                                                part_lo[:, cols], start=False, stop=True)
                    last.then_inc(a_full, 1)
                pe.wait_ge(v_free, VEC_AT["wvo"] + 1)
                o = ab(("v", b))
                for n in range(TPB):
                    last = nc.tensor.matmul(o[:, n // 4, (n % 4) * P:(n % 4 + 1) * P],
                                            xnT[:, (t0 + n) * P:(t0 + n + 1) * P], wvoT[:, 0, :],
                                            start=True, stop=True)
                last.then_inc(a_full, 1)

            pe.wait_ge(ld_lora, 64)
            o = vb("lora_u")
            for j in range(HC):
                last = nc.tensor.transpose(o[0:RANK, j * P:(j + 1) * P], u_sb[:, j, :], ident)
            last.then_inc(v_full, 1)
            pe.wait_ge(v_free, VEC_AT["lora_u"] + 1)
            nc.tensor.matmul(vb("lora_b")[0:RANK, :], fb_sb[:, :], uT[:, :], start=True,
                             stop=True).then_inc(v_full, 1)
            pe.wait_ge(w1_ready, 1)
            pe.wait_ge(v_free, VEC_AT["lora_b"] + 1)
            o = vb("w1")
            for j in range(HC):
                nc.tensor.matmul(o[:, j * P:(j + 1) * P], wfc_sb[:, j, :], ident, start=True, stop=False)
                last = nc.tensor.matmul(o[:, j * P:(j + 1) * P], v_sb[:, :], loraB[:, j * P:(j + 1) * P], start=False, stop=True)
            last.then_inc(v_full, 1)
            pe.wait_ge(w2_ready, 1)
            o = vb("w2")
            for j in range(HC):
                last = nc.tensor.transpose(o[:, j * P:(j + 1) * P], wpj_sb[:, j * P:(j + 1) * P], ident)
            last.then_inc(v_full, 1)
            pe.wait_ge(a_free, len(ACT_PREP))
            pe.wait_ge(v_free, len(VEC_PREP))

            for item in ORDER:
                kind = item[0]
                if kind == "ffn":
                    b, j = item[1] // HC, item[1] % HC
                    o = ab(item)
                    for k in range(2):
                        last = nc.tensor.matmul(o[:, k, :], w1T[:, j * P:(j + 1) * P],
                                                xnT[:, b * T + k * CH:b * T + (k + 1) * CH], start=True, stop=True)
                    last.then_inc(a_full, 1)
                elif kind == "max":
                    c = item[1]
                    b, g, chunk = coords(c)
                    i, half, h, keys = max_units(c)[item[2]]
                    o = vb(item)
                    q0, k0 = b * T + i * P, b * T + half * CH
                    r = slice(32 * h, 32 * h + 32)
                    last = nc.tensor.matmul(o[:, 0:keys], Qr[r, g, q0:q0 + P], Kr[r, g, k0:k0 + keys],
                                            start=True, stop=half < chunk)
                    if half == chunk:
                        last = nc.tensor.matmul(o[:, keys - P:keys], ident16[:, :], mask16[:, :],
                                                start=False, stop=True)
                    last.then_inc(v_full, 1)
                elif kind == "maxT":
                    c = item[1]
                    o = vb(item)
                    pe.wait_ge(prep_ready, c + 1)
                    for n in range(TPC):
                        last = nc.tensor.matmul(o[:, n * P:(n + 1) * P],
                                                M16[:, c % 2, n, :, :].rearrange("p j r -> p (j r)"), ident16[:, :],
                                                start=True, stop=True)
                    last.then_inc(v_full, 1)
                elif kind == "st":
                    _, c, step, pair = item
                    b, g, chunk = coords(c)
                    j, first, cols = steps(c)[step]
                    o = ab(item)
                    if step == 0 and pair == 0:
                        pe.wait_ge(v_free, VEC_AT[("maxT", c, 0)] + 1)
                    q0, k0 = b * T + chunk * CH + first, b * T + j * P
                    for n in range(2):
                        r = slice(32 * (2 * pair + n), 32 * (2 * pair + n) + 32)
                        diag = j >= TPC * chunk
                        last = nc.tensor.matmul(o[:, n, 0:cols], Kr[r, g, k0:k0 + P], Qr[r, g, q0:q0 + cols],
                                                start=True, stop=not diag)
                        if diag:
                            last = nc.tensor.matmul(o[:, n, 0:P], mask16[:, :], ident16[:, :],
                                                    start=False, stop=True)
                    last.then_inc(a_full, 1)
                elif kind == "pv":
                    _, c, step = item
                    b, g, chunk = coords(c)
                    j, first, cols = steps(c)[step]
                    n = STEP0[c] + step
                    if step == 0 and c >= 2:
                        pe.wait_ge(norm_done, c - 1)
                    pe.wait_ge(a_free, ACT_AT[("st", c, step, 1)] + 1)
                    for h in range(HG):
                        last = nc.tensor.matmul(obank[c % 2][32 * h:32 * h + 32, first:CH],
                                                V[:, b * TPB + j, HG * g + h, :], Pr[:, n % PSLOTS, h, 0:cols],
                                                start=step == 0, stop=step == len(steps(c)) - 1)
                    last.then_inc(pv_done, 1)
                elif kind == "y":
                    _, b, chunk = item
                    o = vb(item)
                    pe.wait_ge(norm_done, (b * G + G - 1) * NCH + chunk + 1)
                    pe.wait_ge(r2_ready, (b + 1) * HC)
                    for n in range(TPC):
                        t = slice(b * T + chunk * CH + n * P, b * T + chunk * CH + (n + 1) * P)
                        dst = o[:, n * P:(n + 1) * P]
                        for g in range(G):
                            nc.tensor.matmul(dst, on[:, g, t], wvoT[:, 1 + g, :], start=g == 0, stop=False)
                        for j in range(HC):
                            last = nc.tensor.matmul(dst, r2[:, j, t], w2T[:, j, :], start=False, stop=j == HC - 1)
                    last.then_inc(v_full, 1)


_INS = ["L0_attn_x", "L0_attn_Wq", "L0_attn_Wk", "L0_attn_Wv", "L0_attn_Wo", "L0_attn_scale", "L0_ffn_fast_b",
        "L0_ffn_w_fc", "L0_ffn_w_proj", "L0_ffn_u", "L0_ffn_v", "L0_ffn_gate"]


def kernel(**inputs):
    import numpy as _np
    import concourse.bacc as _bacc
    from concourse import mybir as _mybir
    from concourse.bass_utils import run_bass_kernel_spmd as _run

    nc = _bacc.Bacc("TRN2", target_bir_lowering=False, num_devices=1)
    arrays, args = {}, []
    for name in _INS:
        a = _np.ascontiguousarray(inputs[name])
        if a.ndim == 0:
            a = a.reshape(1, 1)
        arrays[f"in_{name}"] = a
        args.append(nc.dram_tensor(f"in_{name}", a.shape, _mybir.dt.from_np(a.dtype), kind="ExternalInput").ap())
    k = constants()
    arrays["in_consts"] = k
    args.append(nc.dram_tensor("in_consts", k.shape, _mybir.dt.float32, kind="ExternalInput").ap())
    args.append(nc.dram_tensor("out_y", (B, T, C), _mybir.dt.float32, kind="ExternalOutput").ap())
    build(nc, *args)
    r = _run(nc, [arrays], core_ids=[0])
    return r.results[0]["out_y"]
```

```python
import concourse.bass as bass
from concourse import mybir
from contextlib import ExitStack
import numpy as np

B, T, C, H = 2, 1024, 128, 8
HD = C // H
HID, RANK = 512, 16
P = 128
NT = B * T // P
TPB = T // P
HG = 4
G = H // HG
CH = 512
NCH = T // CH
TPC = CH // P
NC = B * G * NCH
HC = HID // P
NPART = 3
NQ = 3 * H
MROW = 3 * NPART * NPART
NEG = -1.0e30
LN_EPS = 1e-05
MIN_SCALE = 1e-05
PSLOTS = 4

CID, CMASK, CSEL = 0, P, 2 * P
CDIR = CSEL + 8 * P
CONE = CDIR + NQ
CEND = CONE + 1


def constants():
    k = np.zeros((P, CEND), np.float32)
    k[:, CID:CID + P] = np.eye(P)
    k[:, CMASK:CMASK + P] = np.where(np.arange(P)[None, :] > np.arange(P)[:, None], NEG, 0.0)
    for g in range(G):
        for j in range(HG):
            for i in range(NPART):
                for n in range(NPART):
                    for d in range(3):
                        col = 32 * j + 3 * (NPART * i + n) + d
                        comp = 3 * (HG * g + j) + d
                        for side, part, row in ((0, i, comp), (1, n, NQ + comp)):
                            low = part == 2
                            at = CSEL + ((2 * side + low) * G + g) * P + col
                            k[row if low else row + 64 * part, at] = 1.0
    signs = np.array([[-1.0 if not (h >> (2 - d)) & 1 else 1.0 for d in range(3)] for h in range(H)], np.float32)
    dirs = signs / np.linalg.norm(signs, axis=1, keepdims=True)
    for h in range(H):
        k[3 * h:3 * h + 3, CDIR + 3 * h:CDIR + 3 * h + 3] = np.outer(dirs[h], dirs[h])
    for j in range(HG):
        k[32 * j + MROW:32 * j + MROW + NPART, CONE] = 1.0
    return k


def coords(c):
    return c // (G * NCH), c // NCH % G, c % NCH


def max_units(c):
    chunk = coords(c)[2]
    units = []
    for i in range(TPC * chunk, TPC * (chunk + 1)):
        for half in range(chunk + 1):
            keys = min(CH, P * (i + 1) - CH * half)
            heads = CH // keys
            units += [(i, half, h, heads, keys) for h in range(0, HG, heads)]
    return units


def steps(c):
    chunk = coords(c)[2]
    out = []
    for j in range(TPC * (chunk + 1)):
        first = max(0, P * (j - TPC * chunk))
        out.append((j, first, CH - first))
    return out


STEP0 = [sum(len(steps(k)) for k in range(c)) for c in range(NC + 1)]


def schedule():
    vec = []
    for c in range(NC):
        units = [("max", c, u) for u in range(len(max_units(c)))]
        vec += units[:4] + ([("maxT", c - 1)] if c else []) + units[4:] + [("prep", c)]
    vec.append(("maxT", NC - 1))
    act = [("ffn", f) for f in range(B * HC)]
    last = None
    for c in range(NC):
        for n in range(len(steps(c))):
            act += [("st", c, n, 0), ("st", c, n, 1)]
            if last:
                act.append(("pv",) + last)
            last = (c, n)
    act.append(("pv",) + last)
    order = [("load", k, side) for k in range(G) for side in range(2)]
    tv, ta, ready, late = 0.0, 0.0, {}, []
    while vec or act:
        item = act[0] if act else None
        free = item is not None and (item[0] != "st" or item[1] in ready)
        if free and item[0] == "st":
            ta = max(ta, ready[item[1]])
        if free and (not vec or ta <= tv):
            item = act.pop(0)
        else:
            item = vec.pop(0)
        order.append(item)
        kind, c = item[0], item[1]
        for x in late:
            x[0] -= 1
        if kind == "ffn":
            ta += 1700
        elif kind == "st":
            ta += 72 + 0.833 * 2 * steps(c)[item[2]][2]
            if item[2:] == (len(steps(c)) - 1, 1) and c % NCH == NCH - 1 and c // NCH + G < B * G:
                order.append(("load", c // NCH + G, 1))
        elif kind == "max":
            u = max_units(c)[item[2]]
            tv += 67 + 1.04 * u[3] * u[4]
            if item[2] == len(max_units(c)) - 1 and c % NCH == NCH - 1 and c // NCH + G < B * G:
                order.append(("load", c // NCH + G, 0))
        elif kind == "maxT":
            tv += 600
            ready[c] = tv + 500
        elif kind == "pv" and item[2] == len(steps(c)) - 1:
            b, g, chunk = coords(c)
            late += [[2, ("ocopy", c)], [6, ("oT", c)]]
            tv += 1200
            if g == G - 1:
                late += [[11, ("oB", b, chunk)], [16, ("y", b, chunk)]]
        while late and min(late)[0] <= 0:
            x = min(late, key=lambda x: x[0])
            late.remove(x)
            order.append(x[1])
    return order + [x[1] for x in sorted(late, key=lambda x: x[0])]


ORDER = schedule()
VEC_PREP = ["wqk", "wvo", "lora_u", "lora_b", "w1", "w2"]
ACT_PREP = [(kind, b) for b in range(B) for kind in ("xT", "qk", "sel0", "sel1", "sel2", "sel3", "v")]
VEC_UNITS = VEC_PREP + [x for x in ORDER if x[0] in ("max", "maxT", "oT", "oB", "y")]
ACT_UNITS = ACT_PREP + [x for x in ORDER if x[0] in ("ffn", "st")]
VEC_AT = {x: n for n, x in enumerate(VEC_UNITS)}
ACT_AT = {x: n for n, x in enumerate(ACT_UNITS)}


def build(nc, x, Wq, Wk, Wv, Wo, scale, fast_b, w_fc, w_proj, u, v, gate, consts, out):
    f32, bf16 = mybir.dt.float32, mybir.dt.bfloat16
    ALU, ACT, AX = mybir.AluOpType, mybir.ActivationFunctionType, mybir.AxisListType
    ctx = ExitStack()
    with ctx:
        def sb(name, shape, dt=f32):
            return ctx.enter_context(nc.sbuf_tensor(name, shape, dt))

        def ps(name, shape):
            return ctx.enter_context(nc.psum_tensor(name, shape, f32))

        def sem(name):
            return ctx.enter_context(nc.semaphore(name))

        x_sb = sb("x_sb", [P, NT, C])
        xn = sb("xn", [P, NT, C])
        xnT = sb("xnT", [P, B * T])
        k_sb = sb("k_sb", [P, CEND])
        ident = k_sb[:, CID:CID + P]
        ident16 = sb("ident16", [P, P], bf16)
        mask16 = sb("mask16", [P, P], bf16)
        sel16 = sb("sel16", [P, 8, P], bf16)
        Wq_sb, Wk_sb = sb("Wq_sb", [NQ, C]), sb("Wk_sb", [NQ, C])
        Wv_sb, Wo_sb = sb("Wv_sb", [P, C]), sb("Wo_sb", [P, C])
        scale_c, gate_c = sb("scale_c", [NQ, 1]), sb("gate_c", [RANK, 1])
        mix = sb("mix", [NQ, NQ])
        wqkT = sb("wqkT", [P, 2 * NQ])
        wvoT = sb("wvoT", [P, 2, P])
        wfc_sb, wpj_sb = sb("wfc_sb", [P, HC, C]), sb("wpj_sb", [P, HID])
        u_sb, v_sb = sb("u_sb", [P, HC, RANK]), sb("v_sb", [RANK, C])
        fb_sb = sb("fb_sb", [RANK, RANK])
        loraB, uT = sb("loraB", [RANK, HID]), sb("uT", [RANK, HID])
        fc_sc, pj_sc = sb("fc_sc", [P, 3, HC]), sb("pj_sc", [P, 3])
        w1T, w2T = sb("w1T", [P, HID]), sb("w2T", [P, HC, C])
        stats, mv = sb("stats", [P, NT, 6]), sb("mv", [P, NT, 2])
        var, std, rstd, nwt = sb("var", [P, NT]), sb("std", [P, NT]), sb("rstd", [P, NT]), sb("nwt", [P, NT])
        Pr = sb("Pr", [P, PSLOTS, HG, CH])
        qk32, res = (Pr[0:2 * NQ, n, :, :].rearrange("p h n -> p (h n)") for n in range(2))
        part_hm, part_lo = sb("part_hm", [P, B * T], bf16), sb("part_lo", [2 * NQ, B * T], bf16)
        Qr, Kr = sb("Qr", [P, G, B * T], bf16), sb("Kr", [P, G, B * T], bf16)
        Qz, Kz = sb("Qz", [P, G, HG, T], bf16), sb("Kz", [P, G, HG, T], bf16)
        V = sb("V", [P, NT, H, 32])
        r2 = sb("r2", [P, HC, B * T])
        tern = r2[:, 0, :].rearrange("p (w s j c) -> p w s j c", w=2, s=2, j=HC)
        pm = sb("pm", [P, 2, 2, TPC, HG])
        nmax, nres = sb("nmax", [P, 2, TPC, HG]), sb("nres", [P, TPC, HG])
        M16 = sb("M16", [P, 2, TPC, HG, 32], bf16)
        oT = sb("oT", [P, 2, CH])
        inv = sb("inv", [P, TPC, HG])
        on = sb("on", [P, 2, TPC, G, HG, HD])
        onT = sb("onT", [P, 2, CH])
        y_sb = xn

        vbank = [ps(f"vbank{i}", [P, CH]) for i in range(2)]
        abank = [ps(f"abank{i}", [P, 2, CH]) for i in range(2)]
        obank = [ps(f"obank{i}", [P, CH]) for i in range(2)]

        ld_x = [sem(f"ld_x{i}") for i in range(4)]
        ld_id, ld_k, ld_qk, ld_vo, ld_fc, ld_pj, ld_lora = (
            sem(n) for n in ("ld_id", "ld_k", "ld_qk", "ld_vo", "ld_fc", "ld_pj", "ld_lora"))
        v_full, v_free, a_full, a_free = (sem(n) for n in ("v_full", "v_free", "a_full", "a_free"))
        qz_ready, kz_ready = [sem(f"qz_ready{i}") for i in range(2)], [sem(f"kz_ready{i}") for i in range(2)]
        o_copied = sem("o_copied")
        dve_chain, pool_chain = sem("dve_chain"), sem("pool_chain")
        mix_ready, heads_zero, casts_ready, zeros_ready = (
            sem(n) for n in ("mix_ready", "heads_zero", "casts_ready", "zeros_ready"))
        var_ready, std_ready, xn_ready = sem("var_ready"), sem("std_ready"), sem("xn_ready")
        hi_ready, res_ready, mid_ready, lo_ready = (
            sem(n) for n in ("hi_ready", "res_ready", "mid_ready", "lo_ready"))
        fc_signs, pj_signs, w1_ready, w2_ready = (sem(n) for n in ("fc_signs", "pj_signs", "w1_ready", "w2_ready"))
        r2_ready, maxima_ready, prep_ready, pv_done, stored = (
            sem(n) for n in ("r2_ready", "maxima_ready", "prep_ready", "pv_done", "stored"))

        block = ctx.enter_context(nc.Block())

        @block.sync
        def _(sp):
            xv = x.rearrange("b (n p) c -> p (b n) c", p=P)
            q = NT // 4
            sp.dma_start(k_sb[:, CID:CID + P], consts[:, CID:CID + P]).then_inc(ld_id, 16)
            for i in range(4):
                sp.dma_start(x_sb[:, q * i:q * (i + 1), :], xv[:, q * i:q * (i + 1), :]).then_inc(ld_x[i], 16)
            sp.dma_start(k_sb[:, P:CEND], consts[:, P:CEND]).then_inc(ld_k, 16)
            sp.dma_start(wfc_sb[:, :, :], w_fc.rearrange("(j p) c -> p j c", p=P)).then_inc(ld_fc, 16)
            sp.dma_start(wpj_sb[:, :], w_proj).then_inc(ld_pj, 16)
            n = 0
            sp.wait_ge(heads_zero, 2)
            for item in ORDER:
                if item[0] == "load":
                    _, k, side = item
                    b, g = k // G, k % G
                    sp.wait_ge(a_free, ACT_AT[(f"sel{2 * g + side}", b)] + 1)
                    if k >= G and side == 0:
                        c = (k - G) * NCH + NCH - 1
                        sp.wait_ge(v_full, VEC_AT[("max", c, len(max_units(c)) - 1)] + 1)
                    elif k >= G:
                        c = (k - G) * NCH + NCH - 1
                        sp.wait_ge(a_full, ACT_AT[("st", c, len(steps(c)) - 1, 1)] + 1)
                    src, dst, ready = ((Qr, Qz, qz_ready), (Kr, Kz, kz_ready))[side]
                    for h in range(HG):
                        r = slice(32 * h, 32 * h + 32)
                        sp.dma_start(dst[r, g, h, :], src[r, g, b * T:(b + 1) * T]).then_inc(ready[g], 16)
                elif item[0] == "y":
                    _, b, chunk = item
                    sp.wait_ge(v_free, VEC_AT[item] + 1)
                    t0 = b * TPB + chunk * TPC
                    ov = out.rearrange("b (n p) c -> p (b n) c", p=P)
                    sp.dma_start(ov[:, t0:t0 + TPC, :], y_sb[:, t0:t0 + TPC, :]).then_inc(stored, 16)
                    n += 1
            sp.wait_ge(stored, 16 * n)

        @block.gpsimd
        def _(pool):
            chain = [0]

            def link(ins):
                chain[0] += 1
                ins.then_inc(pool_chain, 1)
                pool.wait_ge(pool_chain, chain[0])

            pool.dma_start(Wq_sb[:, :], Wq).then_inc(ld_qk, 16)
            pool.dma_start(Wk_sb[:, :], Wk).then_inc(ld_qk, 16)
            pool.dma_start(scale_c[:, :], scale.to_broadcast([NQ, 1])).then_inc(ld_qk, 16)
            pool.dma_start(Wv_sb[:, :], Wv).then_inc(ld_vo, 16)
            pool.dma_start(Wo_sb[:, :], Wo).then_inc(ld_vo, 16)
            pool.dma_start(u_sb[:, :, :], u.rearrange("(j p) r -> p j r", p=P)).then_inc(ld_lora, 16)
            pool.dma_start(v_sb[:, :], v).then_inc(ld_lora, 16)
            pool.dma_start(fb_sb[:, :], fast_b).then_inc(ld_lora, 16)
            pool.dma_start(gate_c[:, :], gate.to_broadcast([RANK, 1])).then_inc(ld_lora, 16)
            nc.gpsimd.memset(part_hm[:, :], 0.0).then_inc(zeros_ready, 1)
            for z in (Qz, Kz):
                nc.gpsimd.memset(z[:, :, :, :].rearrange("p g h t -> p (g h t)").bitcast(f32), 0.0
                                 ).then_inc(heads_zero, 1)
            nc.gpsimd.memset(V[:, :, :, HD:32], 1.0).then_inc(zeros_ready, 1)
            nc.gpsimd.memset(M16[:, :, :, :, :], 0.0).then_inc(zeros_ready, 1)
            pool.wait_ge(zeros_ready, 3)

            wp = wpj_sb[:, :].rearrange("p (j c) -> p j c", j=HC)
            for k, (w, sc, signs, ready) in enumerate((
                    (wfc_sb[:, :, :], fc_sc[:, 0, :, None].to_broadcast([P, HC, C]), fc_signs, w1_ready),
                    (wp, pj_sc[:, 0:1, None].to_broadcast([P, HC, C]), pj_signs, w2_ready))):
                pool.wait_ge(signs, 2)
                above, below = tern[:, k, 0, :, :], tern[:, k, 1, :, :]
                link(nc.gpsimd.tensor_tensor(above, above, below, ALU.subtract))
                link(nc.gpsimd.tensor_tensor(below, above, w, ALU.subtract))
                link(nc.gpsimd.tensor_tensor(below, below, w, ALU.add))
                nc.gpsimd.tensor_tensor(w, below, sc, ALU.mult).then_inc(ready, 1)

            for item in ORDER:
                if item[0] == "ffn":
                    f = item[1]
                    b, j = f // HC, f % HC
                    r = r2[:, j, b * T:(b + 1) * T]
                    pool.wait_ge(a_free, ACT_AT[item] + 1)
                    nc.gpsimd.tensor_tensor(r, r, r, ALU.mult).then_inc(r2_ready, 1)
                elif item[0] == "prep":
                    c = item[1]
                    s = c % 2
                    pool.wait_ge(maxima_ready, c + 1)
                    if c >= 2:
                        pool.wait_ge(v_full, VEC_AT[("maxT", c - 2)] + 1)
                    neg = nmax[:, s, :, :]
                    m = [M16[:, s, :, :, MROW + k] for k in range(NPART)]
                    link(nc.gpsimd.tensor_copy(m[0], neg))
                    link(nc.gpsimd.tensor_tensor(nres[:, :, :], neg, m[0], ALU.subtract))
                    link(nc.gpsimd.tensor_copy(m[1], nres[:, :, :]))
                    nc.gpsimd.tensor_tensor(m[2], nres[:, :, :], m[1], ALU.subtract).then_inc(prep_ready, 1)
                    pool.wait_ge(prep_ready, c + 1)

        @block.vector
        def _(dve):
            chain = [0]

            def link(ins):
                chain[0] += 1
                ins.then_inc(dve_chain, 1)
                dve.wait_ge(dve_chain, chain[0])

            def full(unit):
                dve.wait_ge(v_full, VEC_AT[unit] + 1)

            dve.wait_ge(ld_qk, 48)
            dve.wait_ge(ld_id, 16)
            dve.wait_ge(ld_k, 16)
            nc.vector.scalar_tensor_tensor(out=mix[:, :], in0=k_sb[0:NQ, CID:CID + NQ], scalar=scale_c[:, 0:1],
                                           in1=k_sb[0:NQ, CDIR:CDIR + NQ], op0=ALU.mult,
                                           op1=ALU.add).then_inc(mix_ready, 1)
            nc.vector.tensor_copy(ident16[:, :], k_sb[:, CID:CID + P]).then_inc(casts_ready, 1)
            nc.vector.tensor_copy(mask16[:, :], k_sb[:, CMASK:CMASK + P]).then_inc(casts_ready, 1)
            nc.vector.tensor_copy(sel16[:, :, :], k_sb[:, CSEL:CDIR].rearrange("p (s c) -> p s c", c=P)
                                  ).then_inc(casts_ready, 1)

            def variances(b):
                t0 = b * TPB
                for n in range(t0, t0 + TPB):
                    if n % 4 == 0:
                        dve.wait_ge(ld_x[n // 4], 16)
                    last = nc.vector.bn_stats(stats[:, n, :], x_sb[:, n, :])
                link(last)
                for n in range(t0, t0 + TPB):
                    last = nc.vector.bn_aggr(mv[:, n, :], stats[:, n, :])
                link(last)
                nc.vector.tensor_scalar(var[:, t0:t0 + TPB], mv[:, t0:t0 + TPB, 1], LN_EPS, None,
                                        ALU.add).then_inc(var_ready, 1)

            def normalise(b):
                t0 = b * TPB
                s = slice(t0, t0 + TPB)
                dve.wait_ge(std_ready, b + 1)
                link(nc.vector.reciprocal(rstd[:, s], std[:, s]))
                link(nc.vector.tensor_tensor(nwt[:, s], rstd[:, s], rstd[:, s], ALU.mult))
                link(nc.vector.tensor_tensor(nwt[:, s], nwt[:, s], var[:, s], ALU.mult))
                link(nc.vector.tensor_scalar(nwt[:, s], nwt[:, s], -0.5, 1.5, ALU.mult, ALU.add))
                link(nc.vector.tensor_tensor(rstd[:, s], rstd[:, s], nwt[:, s], ALU.mult))
                for n in range(t0, t0 + TPB):
                    last = nc.vector.tensor_scalar(xn[:, n, :], x_sb[:, n, :], mv[:, n, 0:1], rstd[:, n:n + 1],
                                                   ALU.subtract, ALU.mult)
                last.then_inc(xn_ready, 1)

            def subtract_first(b):
                cols = slice(b * T, (b + 1) * T)
                dve.wait_ge(hi_ready, b + 1)
                dve.wait_ge(a_free, ACT_AT[("qk", b)] + 1)
                nc.vector.tensor_tensor(res[:, cols], qk32[:, cols], part_hm[0:2 * NQ, cols],
                                        ALU.subtract).then_inc(res_ready, 1)

            def last_parts(b):
                cols = slice(b * T, (b + 1) * T)
                dve.wait_ge(mid_ready, b + 1)
                nc.vector.tensor_tensor(part_lo[:, cols], res[:, cols], part_hm[64:64 + 2 * NQ, cols],
                                        ALU.subtract).then_inc(lo_ready, 1)

            variances(0)
            normalise(0)
            full("wqk")
            nc.vector.tensor_copy(wqkT[:, :], vbank[0][:, 0:2 * NQ]).then_inc(v_free, 1)
            full("wvo")
            nc.vector.tensor_copy(wvoT[:, :, :], vbank[1][:, 0:2 * P].rearrange("p (k c) -> p k c", c=P)
                                  ).then_inc(v_free, 1)
            variances(1)
            subtract_first(0)
            last_parts(0)
            normalise(1)
            dve.wait_ge(ld_fc, 16)
            link(nc.vector.tensor_reduce(out=fc_sc[:, 1, :], in_=wfc_sb[:, :, :], op=ALU.add, axis=AX.X,
                                         apply_absolute_value=True))
            link(nc.vector.tensor_scalar(fc_sc[:, 0, :], fc_sc[:, 1, :], 1.0 / C, MIN_SCALE,
                                         ALU.mult, ALU.max))
            nc.vector.tensor_scalar(fc_sc[:, 1, :], fc_sc[:, 0, :], 0.5, None, ALU.mult)
            link(nc.vector.tensor_scalar(fc_sc[:, 2, :], fc_sc[:, 0, :], -0.5, None, ALU.mult))
            for k, op in enumerate((ALU.is_gt, ALU.is_lt)):
                nc.vector.tensor_tensor(tern[:, 0, k, :, :], wfc_sb[:, :, :],
                                        fc_sc[:, 1 + k, :, None].to_broadcast([P, HC, C]),
                                        op).then_inc(fc_signs, 1)
            dve.wait_ge(ld_pj, 16)
            link(nc.vector.tensor_reduce(out=pj_sc[:, 1:2], in_=wpj_sb[:, :], op=ALU.add, axis=AX.X,
                                         apply_absolute_value=True))
            link(nc.vector.tensor_scalar(pj_sc[:, 0:1], pj_sc[:, 1:2], 1.0 / HID, MIN_SCALE,
                                         ALU.mult, ALU.max))
            nc.vector.tensor_scalar(pj_sc[:, 1:2], pj_sc[:, 0:1], 0.5, None, ALU.mult)
            link(nc.vector.tensor_scalar(pj_sc[:, 2:3], pj_sc[:, 0:1], -0.5, None, ALU.mult))
            for k, op in enumerate((ALU.is_gt, ALU.is_lt)):
                nc.vector.tensor_scalar(tern[:, 1, k, :, :].rearrange("p j c -> p (j c)"), wpj_sb[:, :],
                                        pj_sc[:, 1 + k:2 + k], None, op).then_inc(pj_signs, 1)
            subtract_first(1)
            last_parts(1)
            full("lora_u")
            nc.vector.tensor_copy(uT[:, :], vbank[0][0:RANK, :]).then_inc(v_free, 1)
            full("lora_b")
            nc.vector.tensor_scalar(loraB[:, :], vbank[1][0:RANK, :], gate_c[:, 0:1], None,
                                    ALU.mult).then_inc(v_free, 1)
            full("w1")
            nc.vector.tensor_copy(w1T[:, :], vbank[0][:, :]).then_inc(v_free, 1)
            full("w2")
            nc.vector.tensor_copy(w2T[:, :, :], vbank[1][:, :].rearrange("p (j c) -> p j c", j=HC)
                                  ).then_inc(v_free, 1)

            for item in ORDER:
                kind = item[0]
                if kind == "max":
                    c = item[1]
                    i, half, h, heads, keys = max_units(c)[item[2]]
                    if item[2] == 0 and c >= 2:
                        dve.wait_ge(prep_ready, c - 1)
                    full(item)
                    src = vbank[VEC_AT[item] % 2][:, 0:heads * keys].rearrange("p (h k) -> p h k", h=heads)
                    nc.vector.tensor_reduce(out=pm[:, c % 2, half, i % TPC, h:h + heads], in_=src, op=ALU.max,
                                            axis=AX.X, negate=True).then_inc(v_free, 1)
                elif kind == "prep":
                    c = item[1]
                    dve.wait_ge(v_free, VEC_AT[("max", c, len(max_units(c)) - 1)] + 1)
                    nc.vector.tensor_tensor(nmax[:, c % 2, :, :], pm[:, c % 2, 0, :, :],
                                            pm[:, c % 2, coords(c)[2], :, :], ALU.min).then_inc(maxima_ready, 1)
                elif kind == "maxT":
                    c = item[1]
                    b, g, chunk = coords(c)
                    q = Qr[:, g, b * T + chunk * CH:b * T + (chunk + 1) * CH]
                    full(item)
                    nc.vector.tensor_tensor(q, vbank[VEC_AT[item] % 2][:, :], q, ALU.add).then_inc(v_free, 1)
                elif kind == "oT":
                    c = item[1]
                    b, g, chunk = coords(c)
                    full(item)
                    o = vbank[VEC_AT[item] % 2][:, :].rearrange("p (n h r) -> p n h r", n=TPC, h=HG)
                    link(nc.vector.reciprocal(inv[:, :, :], o[:, :, :, HD]))
                    if b and g == 0:
                        dve.wait_ge(v_full, VEC_AT[("oB", b - 1, chunk)] + 1)
                    nc.vector.tensor_tensor(on[:, chunk, :, g, :, :], o[:, :, :, 0:HD],
                                            inv[:, :, :, None].to_broadcast([P, TPC, HG, HD]),
                                            ALU.mult).then_inc(v_free, 1)
                elif kind == "oB":
                    full(item)
                    nc.vector.tensor_copy(onT[:, item[2], :], vbank[VEC_AT[item] % 2][:, :]).then_inc(v_free, 1)
                elif kind == "y":
                    _, b, chunk = item
                    t0 = b * TPB + chunk * TPC
                    full(item)
                    src = vbank[VEC_AT[item] % 2][:, :].rearrange("p (n c) -> p n c", n=TPC)
                    nc.vector.tensor_tensor(y_sb[:, t0:t0 + TPC, :], src, x_sb[:, t0:t0 + TPC, :],
                                            ALU.add).then_inc(v_free, 1)

        @block.scalar
        def _(act):
            def full(unit):
                act.wait_ge(a_full, ACT_AT[unit] + 1)

            def deviations(b):
                act.wait_ge(var_ready, b + 1)
                nc.scalar.activation(std[:, b * TPB:(b + 1) * TPB], var[:, b * TPB:(b + 1) * TPB],
                                     ACT.Sqrt).then_inc(std_ready, 1)

            deviations(0)
            for b in range(B):
                cols = slice(b * T, (b + 1) * T)

                def bank(unit):
                    return abank[ACT_AT[unit] % 2]

                full(("xT", b))
                nc.scalar.copy(xnT[:, cols], bank(("xT", b))[:, :, :].rearrange("p a n -> p (a n)")
                               ).then_inc(a_free, 1)
                full(("qk", b))
                src = bank(("qk", b))[0:2 * NQ, :, :].rearrange("p a n -> p (a n)")
                if b == 0:
                    act.wait_ge(zeros_ready, 3)
                nc.scalar.copy(part_hm[0:2 * NQ, cols], src).then_inc(hi_ready, 1)
                nc.scalar.copy(qk32[:, cols], src).then_inc(a_free, 1)
                if b == 0:
                    deviations(1)
                act.wait_ge(res_ready, b + 1)
                nc.scalar.copy(part_hm[64:64 + 2 * NQ, cols], res[:, cols]).then_inc(mid_ready, 1)
                for s in range(4):
                    g = s // 2
                    unit = (f"sel{s}", b)
                    full(unit)
                    src = bank(unit)[:, :, :].rearrange("p a n -> p (a n)")
                    if s % 2 == 0:
                        nc.scalar.copy(Qr[:, g, cols], src).then_inc(a_free, 1)
                    else:
                        nc.scalar.activation(Kr[:, g, cols], src, ACT.Identity,
                                             bias=k_sb[:, CONE:CONE + 1]).then_inc(a_free, 1)
                full(("v", b))
                nc.scalar.copy(V[:, b * TPB:(b + 1) * TPB, :, 0:HD],
                               bank(("v", b))[:, :, :].rearrange("p a (n h d) -> p (a n) h d", h=H, d=HD)
                               ).then_inc(a_free, 1)

            for item in ORDER:
                if item[0] == "ffn":
                    b, j = item[1] // HC, item[1] % HC
                    full(item)
                    nc.scalar.activation(r2[:, j, b * T:(b + 1) * T],
                                         abank[ACT_AT[item] % 2][:, :, :].rearrange("p a n -> p (a n)"),
                                         ACT.Relu).then_inc(a_free, 1)
                elif item[0] == "ocopy":
                    c = item[1]
                    act.wait_ge(pv_done, STEP0[c + 1])
                    if c >= 2:
                        act.wait_ge(v_full, VEC_AT[("oT", c - 2)] + 1)
                    nc.scalar.copy(oT[:, c % 2, :], obank[c % 2][:, :]).then_inc(o_copied, 1)
                elif item[0] == "st":
                    _, c, step, pair = item
                    n = STEP0[c] + step
                    cols = steps(c)[step][2]
                    if n >= PSLOTS and pair == 0:
                        act.wait_ge(pv_done, n - PSLOTS + 1)
                    full(item)
                    nc.scalar.activation(Pr[:, n % PSLOTS, 2 * pair:2 * pair + 2, 0:cols],
                                         abank[ACT_AT[item] % 2][:, :, 0:cols], ACT.Exp).then_inc(a_free, 1)

        @block.tensor
        def _(pe):
            def vb(unit):
                n = VEC_AT[unit]
                if n >= 2:
                    pe.wait_ge(v_free, n - 1)
                return vbank[n % 2]

            def ab(unit):
                n = ACT_AT[unit]
                if n >= 2:
                    pe.wait_ge(a_free, n - 1)
                return abank[n % 2]

            pe.wait_ge(ld_qk, 48)
            pe.wait_ge(ld_id, 16)
            pe.wait_ge(mix_ready, 1)
            o = vb("wqk")
            nc.tensor.matmul(o[:, 0:NQ], Wq_sb[:, :], mix[:, :], start=True, stop=True)
            nc.tensor.matmul(o[:, NQ:2 * NQ], Wk_sb[:, :], k_sb[0:NQ, CID:CID + NQ], start=True,
                             stop=True).then_inc(v_full, 1)
            pe.wait_ge(ld_vo, 32)
            o = vb("wvo")
            nc.tensor.transpose(o[:, 0:P], Wv_sb[:, :], ident)
            nc.tensor.transpose(o[:, P:2 * P], Wo_sb[:, :], ident).then_inc(v_full, 1)

            for b in range(B):
                t0 = b * TPB
                pe.wait_ge(xn_ready, b + 1)
                o = ab(("xT", b))
                for n in range(TPB):
                    last = nc.tensor.transpose(o[:, n // 4, (n % 4) * P:(n % 4 + 1) * P], xn[:, t0 + n, :], ident)
                last.then_inc(a_full, 1)
                pe.wait_ge(a_free, ACT_AT[("xT", b)] + 1)
                pe.wait_ge(v_free, VEC_AT["wqk"] + 1)
                o = ab(("qk", b))
                for k in range(2):
                    last = nc.tensor.matmul(o[0:2 * NQ, k, :], wqkT[:, :],
                                            xnT[:, b * T + k * CH:b * T + (k + 1) * CH], start=True, stop=True)
                last.then_inc(a_full, 1)
                pe.wait_ge(casts_ready, 3)
                pe.wait_ge(mid_ready, b + 1)
                pe.wait_ge(lo_ready, b + 1)
                for s in range(4):
                    g, side = s // 2, s % 2
                    o = ab((f"sel{s}", b))
                    for k in range(2):
                        cols = slice(b * T + k * CH, b * T + (k + 1) * CH)
                        nc.tensor.matmul(o[:, k, :], sel16[:, 2 * side * G + g, :], part_hm[:, cols],
                                         start=True, stop=False)
                        last = nc.tensor.matmul(o[:, k, :], sel16[0:2 * NQ, (2 * side + 1) * G + g, :],
                                                part_lo[:, cols], start=False, stop=True)
                    last.then_inc(a_full, 1)
                pe.wait_ge(v_free, VEC_AT["wvo"] + 1)
                o = ab(("v", b))
                for n in range(TPB):
                    last = nc.tensor.matmul(o[:, n // 4, (n % 4) * P:(n % 4 + 1) * P],
                                            xnT[:, (t0 + n) * P:(t0 + n + 1) * P], wvoT[:, 0, :],
                                            start=True, stop=True)
                last.then_inc(a_full, 1)

            pe.wait_ge(ld_lora, 64)
            o = vb("lora_u")
            for j in range(HC):
                last = nc.tensor.transpose(o[0:RANK, j * P:(j + 1) * P], u_sb[:, j, :], ident)
            last.then_inc(v_full, 1)
            pe.wait_ge(v_free, VEC_AT["lora_u"] + 1)
            nc.tensor.matmul(vb("lora_b")[0:RANK, :], fb_sb[:, :], uT[:, :], start=True,
                             stop=True).then_inc(v_full, 1)
            pe.wait_ge(w1_ready, 1)
            pe.wait_ge(v_free, VEC_AT["lora_b"] + 1)
            o = vb("w1")
            for j in range(HC):
                nc.tensor.matmul(o[:, j * P:(j + 1) * P], wfc_sb[:, j, :], ident, start=True, stop=False)
                last = nc.tensor.matmul(o[:, j * P:(j + 1) * P], v_sb[:, :], loraB[:, j * P:(j + 1) * P], start=False, stop=True)
            last.then_inc(v_full, 1)
            pe.wait_ge(w2_ready, 1)
            o = vb("w2")
            for j in range(HC):
                last = nc.tensor.transpose(o[:, j * P:(j + 1) * P], wpj_sb[:, j * P:(j + 1) * P], ident)
            last.then_inc(v_full, 1)
            pe.wait_ge(a_free, len(ACT_PREP))
            pe.wait_ge(v_free, len(VEC_PREP))

            for item in ORDER:
                kind = item[0]
                if kind == "ffn":
                    b, j = item[1] // HC, item[1] % HC
                    o = ab(item)
                    for k in range(2):
                        last = nc.tensor.matmul(o[:, k, :], w1T[:, j * P:(j + 1) * P],
                                                xnT[:, b * T + k * CH:b * T + (k + 1) * CH], start=True, stop=True)
                    last.then_inc(a_full, 1)
                elif kind == "max":
                    c = item[1]
                    b, g, chunk = coords(c)
                    i, half, h0, heads, keys = max_units(c)[item[2]]
                    if item[2] == 0 and chunk == 0:
                        pe.wait_ge(qz_ready[(b * G + g) % 2], 16 * HG * ((b * G + g) // 2 + 1))
                    o = vb(item)
                    k0 = b * T + half * CH
                    for n in range(heads):
                        last = nc.tensor.matmul(o[:, n * keys:(n + 1) * keys],
                                                Qz[:, g, h0 + n, i * P:(i + 1) * P], Kr[:, g, k0:k0 + keys],
                                                start=True, stop=half < chunk)
                        if half == chunk:
                            last = nc.tensor.matmul(o[:, (n + 1) * keys - P:(n + 1) * keys], ident16[:, :],
                                                    mask16[:, :], start=False, stop=True)
                    last.then_inc(v_full, 1)
                elif kind == "maxT":
                    c = item[1]
                    o = vb(item)
                    pe.wait_ge(prep_ready, c + 1)
                    for n in range(TPC):
                        last = nc.tensor.matmul(o[:, n * P:(n + 1) * P],
                                                M16[:, c % 2, n, :, :].rearrange("p j r -> p (j r)"), ident16[:, :],
                                                start=True, stop=True)
                    last.then_inc(v_full, 1)
                elif kind == "st":
                    _, c, step, pair = item
                    b, g, chunk = coords(c)
                    j, first, cols = steps(c)[step]
                    o = ab(item)
                    if step == 0 and pair == 0:
                        pe.wait_ge(v_free, VEC_AT[("maxT", c)] + 1)
                        pe.wait_ge(kz_ready[(b * G + g) % 2], 16 * HG * ((b * G + g) // 2 + 1))
                    q0 = b * T + chunk * CH + first
                    for n in range(2):
                        diag = j >= TPC * chunk
                        last = nc.tensor.matmul(o[:, n, 0:cols], Kz[:, g, 2 * pair + n, j * P:(j + 1) * P],
                                                Qr[:, g, q0:q0 + cols],
                                                start=True, stop=not diag)
                        if diag:
                            last = nc.tensor.matmul(o[:, n, 0:P], mask16[:, :], ident16[:, :],
                                                    start=False, stop=True)
                    last.then_inc(a_full, 1)
                elif kind == "pv":
                    _, c, step = item
                    b, g, chunk = coords(c)
                    j, first, cols = steps(c)[step]
                    n = STEP0[c] + step
                    if step == 0 and c >= 2:
                        pe.wait_ge(o_copied, c - 1)
                    pe.wait_ge(a_free, ACT_AT[("st", c, step, 1)] + 1)
                    for h in range(HG):
                        last = nc.tensor.matmul(obank[c % 2][32 * h:32 * h + 32, first:CH],
                                                V[:, b * TPB + j, HG * g + h, :], Pr[:, n % PSLOTS, h, 0:cols],
                                                start=step == 0, stop=step == len(steps(c)) - 1)
                    last.then_inc(pv_done, 1)
                elif kind == "oT":
                    c = item[1]
                    o = vb(item)
                    pe.wait_ge(o_copied, c + 1)
                    for n in range(TPC):
                        last = nc.tensor.transpose(o[:, n * P:(n + 1) * P], oT[:, c % 2, n * P:(n + 1) * P], ident)
                    last.then_inc(v_full, 1)
                elif kind == "oB":
                    _, b, chunk = item
                    o = vb(item)
                    pe.wait_ge(v_free, VEC_AT[("oT", (b * G + G - 1) * NCH + chunk)] + 1)
                    for n in range(TPC):
                        last = nc.tensor.transpose(o[:, n * P:(n + 1) * P],
                                                   on[:, chunk, n, :, :, :].rearrange("p g h d -> p (g h d)"), ident)
                    last.then_inc(v_full, 1)
                elif kind == "y":
                    _, b, chunk = item
                    o = vb(item)
                    pe.wait_ge(v_free, VEC_AT[("oB", b, chunk)] + 1)
                    pe.wait_ge(r2_ready, (b + 1) * HC)
                    for n in range(TPC):
                        t = slice(b * T + chunk * CH + n * P, b * T + chunk * CH + (n + 1) * P)
                        dst = o[:, n * P:(n + 1) * P]
                        nc.tensor.matmul(dst, onT[:, chunk, n * P:(n + 1) * P], wvoT[:, 1, :],
                                         start=True, stop=False)
                        for j in range(HC):
                            last = nc.tensor.matmul(dst, r2[:, j, t], w2T[:, j, :], start=False, stop=j == HC - 1)
                    last.then_inc(v_full, 1)


_INS = ["L0_attn_x", "L0_attn_Wq", "L0_attn_Wk", "L0_attn_Wv", "L0_attn_Wo", "L0_attn_scale", "L0_ffn_fast_b",
        "L0_ffn_w_fc", "L0_ffn_w_proj", "L0_ffn_u", "L0_ffn_v", "L0_ffn_gate"]


def kernel(**inputs):
    import numpy as _np
    import concourse.bacc as _bacc
    from concourse import mybir as _mybir
    from concourse.bass_utils import run_bass_kernel_spmd as _run

    nc = _bacc.Bacc("TRN2", target_bir_lowering=False, num_devices=1)
    arrays, args = {}, []
    for name in _INS:
        a = _np.ascontiguousarray(inputs[name])
        if a.ndim == 0:
            a = a.reshape(1, 1)
        arrays[f"in_{name}"] = a
        args.append(nc.dram_tensor(f"in_{name}", a.shape, _mybir.dt.from_np(a.dtype), kind="ExternalInput").ap())
    k = constants()
    arrays["in_consts"] = k
    args.append(nc.dram_tensor("in_consts", k.shape, _mybir.dt.float32, kind="ExternalInput").ap())
    args.append(nc.dram_tensor("out_y", (B, T, C), _mybir.dt.float32, kind="ExternalOutput").ap())
    build(nc, *args)
    r = _run(nc, [arrays], core_ids=[0])
    return r.results[0]["out_y"]
```

```python
import concourse.bass as bass
from concourse import mybir
from contextlib import ExitStack
import numpy as np

B, T, C, H = 2, 1024, 128, 8
HD = C // H
HID, RANK = 512, 16
P = 128
NT = B * T // P
TPB = T // P
HG = 4
G = H // HG
CH = 512
NCH = T // CH
TPC = CH // P
NC = B * G * NCH
HC = HID // P
FP = HC // 2
NPART = 3
NQ = 3 * H
MROW = 3 * NPART * NPART
NEG = -1.0e30
LN_EPS = 1e-05
MIN_SCALE = 1e-05
PSLOTS = 5
TICK, WARM = 3.41, 1.275
VB, AB = 3, 2

CID, CMASK, CSEL = 0, P, 2 * P
CDIR = CSEL + 8 * P
CONE = CDIR + NQ
CEND = CONE + 1


def constants():
    k = np.zeros((P, CEND), np.float32)
    k[:, CID:CID + P] = np.eye(P)
    k[:, CMASK:CMASK + P] = np.where(np.arange(P)[None, :] > np.arange(P)[:, None], NEG, 0.0)
    for g in range(G):
        for j in range(HG):
            for i in range(NPART):
                for n in range(NPART):
                    for d in range(3):
                        col = 32 * j + 3 * (NPART * i + n) + d
                        comp = 3 * (HG * g + j) + d
                        for side, part, row in ((0, i, comp), (1, n, NQ + comp)):
                            low = part == 2
                            at = CSEL + ((2 * side + low) * G + g) * P + col
                            k[row if low else row + 64 * part, at] = 1.0
    signs = np.array([[-1.0 if not (h >> (2 - d)) & 1 else 1.0 for d in range(3)] for h in range(H)], np.float32)
    dirs = signs / np.linalg.norm(signs, axis=1, keepdims=True)
    for h in range(H):
        k[3 * h:3 * h + 3, CDIR + 3 * h:CDIR + 3 * h + 3] = np.outer(dirs[h], dirs[h])
    for j in range(HG):
        k[32 * j + MROW:32 * j + MROW + NPART, CONE] = 1.0
    return k


def coords(c):
    return c // (G * NCH), c // NCH % G, c % NCH


def max_units(c):
    chunk = coords(c)[2]
    units = []
    for i in range(TPC * chunk, TPC * (chunk + 1)):
        for half in range(chunk + 1):
            keys = min(CH, P * (i + 1) - CH * half)
            heads = CH // keys
            units += [(i, half, h, heads, keys) for h in range(0, HG, heads)]
    return units


def steps(c):
    chunk = coords(c)[2]
    out = []
    for j in range(TPC * (chunk + 1)):
        first = max(0, P * (j - TPC * chunk))
        out.append((j, first, CH - first))
    return out


STEP0 = [sum(len(steps(k)) for k in range(c)) for c in range(NC + 1)]
LAST = B * NCH - 1


def quarter(b, chunk):
    return b * NCH + chunk


def spec(item):
    kind, c = item[0], item[1]
    behind = [(kind, c - 1)] if kind in ("var", "std", "xn", "xT", "qk", "mid", "low", "v") and c else []
    if kind == "x":
        return 0, None, "dma", (3.4, 6.0, 10.5, 11.0)[c], []
    if kind == "fc":
        return 0, None, "dma", (5.5, 8.0)[c], []
    if kind in ("mix", "casts"):
        return 0, None, "dve", {"mix": 0.2, "casts": 1.1}[kind], [("fc", 0)]
    if kind == "weights":
        return {"wqk": (0.4, "v", "dve", 0.15, [("mix", 0)]), "wvo": (0.3, "v", "dve", 0.4, []),
                "lora_u": (0.3, "v", "dve", 0.6, []), "lora_b": (0.9, "v", "dve", 0.6, [("weights", "lora_u")]),
                "w1": (1.8, "v", "dve", 0.6, [("weights", "lora_b"), ("ternary", 0)]),
                "w2": (0.3, "v", "dve", 0.6, [("ternary", 1)])}[c]
    if kind == "ternary":
        return 0, None, "pool", 5.0, [("signs", c)]
    if kind == "signs":
        return 0, None, "dve", 2.5, [("fc", c)]
    if kind == "var":
        return 0, None, "dve", 1.6, [("x", c)] + behind
    if kind == "std":
        return 0, None, "act", 0.3, [("var", c)] + behind
    if kind == "xn":
        return 0, None, "dve", 2.1, [("std", c)] + behind
    if kind == "xT":
        return 0.43, "a", "act", 0.5, [("xn", c)] + behind
    if kind == "qk":
        return 0.86, "v", "dve", 1.2, [("xT", c), ("weights", "wqk")] + behind + \
            ([("mid", c - 2), ("low", c - 2)] if c >= 2 else [])
    if kind == "mid":
        return 0, None, "act", 0.5, [("qk", c)] + behind
    if kind == "low":
        return 0, None, "dve", 0.6, [("mid", c)] + behind
    if kind == "sel":
        return 0.86, "a", "act", 1.05, [("low", c), ("casts", 0)]
    if kind == "direct":
        return 0, None, "dve", 2.1, [("low", 0)]
    if kind == "v":
        return 0.86, "a", "act", 0.5, [("xT", c), ("weights", "wvo")] + behind
    if kind == "load":
        b, g = c // G, c % G
        deps = [("sel", quarter(b, item[2]), g)]
        if c >= G:
            old = (c - G) * NCH + NCH - 1
            deps.append(("st", old, len(steps(old)) - 1, 1))
        return 0, None, "dma", 3.5, deps
    if kind == "ffn":
        return 1.72, "a", "act", 0.93, [("weights", "w1"), ("xT", c // FP)]
    if kind == "square":
        return 0, None, "pool", 2.4, [("ffn", c)]
    if kind == "y0":
        return 0.88, "a" if item[2] == 0 else None, None, 0, \
            [("weights", "w2"), LAST_ST] + [("square", c * FP + j) for j in range(FP)]
    if kind == "y":
        if c == LAST:
            return 0.45, None, "dve", 0.35, [("oB", c)] + [("y0", c, n) for n in range(TPC)]
        return 2.2, "v", "dve", 0.35, [("oB", c), ("weights", "w2")] + [("square", c * FP + j) for j in range(FP)]
    if kind == "oB":
        return 0.43, "v", "dve", 0.6, ([("y", c - NCH, 1)] if c >= NCH else []) + [("oT", (c // NCH * G + G - 1) * NCH + c % NCH)]
    b, g, chunk = coords(c)
    if kind == "max":
        i, half, h, heads, keys = max_units(c)[item[2]]
        deps = [("load", b * G + g, chunk) if c else ("direct", 0), ("casts", 0)] + ([("prep", c - 2)] if c >= 2 else [])
        return heads * (keys / 2400 + 0.003), "v", "dve", 0.075 * (heads if half == chunk else 1) + heads * keys / 960, deps
    if kind == "top":
        return 0, None, "dve", 0.15, [("max", c, len(max_units(c)) - 1)]
    if kind == "prep":
        return 0, None, "pool", 1.3, [("top", c)] + ([("maxT", c - 2)] if c >= 2 else [])
    if kind == "maxT":
        return 0.22, "v", "dve", 0.6, [("prep", c)]
    if kind == "st":
        step, pair = item[2:]
        n, cols = STEP0[c] + step, steps(c)[step][2]
        deps = [("maxT", c)] + [("load", b * G + g, k) for k in range(chunk + 1) if b or g or k]
        if n >= PSLOTS:
            deps.append(("pv",) + STEPS[n - PSLOTS])
        return 2 * (cols / 2400 + 0.003) + (0.11 if steps(c)[step][0] >= TPC * chunk else 0), "a", "act", \
            0.085 + 2 * cols / 1200 + (1.3 if item[1:] == (0, 0, 0) else 0), deps
    if kind == "pv":
        deps = [("st", c, item[2], 1)] + [("v", quarter(b, k)) for k in range(chunk + 1)]
        if item[2] == 0 and c >= 1:
            deps.append(("ocopy", c - 1))
        return 4 * steps(c)[item[2]][2] / 2400 + 0.06, None, None, 0, deps
    if kind == "ocopy":
        return 0, None, "act", 0.5, [("pv", c, len(steps(c)) - 1)] + ([("oT", c - 2)] if c >= 2 else [])
    assert kind == "oT"
    b, g, chunk = coords(c)
    return 0.43, "v", "dve", 0.8, [("ocopy", c), ("weights", "w2")] + \
        ([("oB", quarter(b - 1, chunk))] if b and g == 0 else [])


LAST_ST = ("st", NC - 1, len(steps(NC - 1)) - 1, 1)
STEPS = [(c, n) for c in range(NC) for n in range(len(steps(c)))]


IDLE = {("weights", "wqk"): 12, ("xT", 0): 7, ("qk", 0): 2, ("sel", 0, 0): 6}
PASSED = {"maxima": 0.75, "scores": 0.8, "values": -3.9, "first": -0.5, "second": -0.3, "norms": 0.25, "tokens": 0.5,
          "loads": -1.7, "hidden": 0.7, "project": 1.05, "maxima_T": 0.9, "sums": 0.8, "outs": 0.65}
LEADS = {"maxima": 0.18, "tokens": 0.95, "hidden": 0.89}


def schedule():
    maxima, scores, sums, outs = [], [], [], []
    for c in range(NC):
        maxima += [("max", c, u) for u in range(len(max_units(c)))] + [("top", c), ("prep", c)]
        scores += [("st", c, n, pair) for n in range(len(steps(c))) for pair in range(2)]
        sums += [("pv", c, n) for n in range(len(steps(c)))] + [("ocopy", c)]
        outs.append(("oT", c))
        b, g, chunk = coords(c)
        if g == G - 1:
            q = quarter(b, chunk)
            outs += [("oB", q)] + [("y", q, half) for half in range(2)]
    begun = [("y0", LAST, n) for n in range(TPC)]
    sums = sums[:-2] + [begun[0]] + sums[-2:] + [begun[1], outs[-4], begun[2], outs[-3], begun[3]] + outs[-2:]
    outs = outs[:-4]

    def prologue(q):
        items = [("xT", q), ("qk", q), ("mid", q), ("low", q)]
        for g in range(G):
            items += [("sel", q, g)] + ([("load", g, q)] if 0 < q + g and q < NCH else [])
        return items + [("v", q)]

    quarters = B * NCH
    opening = [("x", q) for q in range(quarters)] + [("fc", 0), ("fc", 1)] \
        + [("var", 0), ("std", 0), ("mix", 0), ("xn", 0), ("weights", "wqk"), ("xT", 0), ("casts", 0), ("signs", 0),
           ("qk", 0), ("mid", 0), ("low", 0), ("ternary", 0), ("sel", 0, 0), ("direct", 0)]
    norms = [item for q in range(1, quarters) for item in (("var", q), ("std", q))]
    early = [prologue(0)[5:], [("xn", 1)] + prologue(1)]
    tokens = [("xn", q) for q in range(NCH, quarters)] + [x for q in range(NCH, quarters) for x in prologue(q)]
    loads = [("load", k, chunk) for k in range(G, B * G) for chunk in range(NCH)]
    hidden = [("weights", "lora_u"), ("weights", "lora_b"), ("weights", "w1")]
    project = [("signs", 1), ("ternary", 1), ("weights", "w2")]
    for f in range(B * NCH * FP):
        hidden += [("ffn", f), ("square", f)]

    order, done = [], {}
    tick = [0.0, 0.0, False]
    clock = {"pe": 1.3, "dve": 0.0, "act": 0.0, "pool": 0.0}
    banks = {"v": [0.0] * VB, "a": [0.0] * AB}
    count = {"v": 0, "a": 0}

    def start(item):
        pe, ring, reader, cost, deps = spec(item)
        if any(d not in done for d in deps):
            return None
        at = max([0.0] + [done[d] for d in deps])
        if pe:
            at = max(at, clock["pe"])
            if ring:
                at = max(at, banks[ring][count[ring] % len(banks[ring])])
        elif reader != "dma":
            at = max(at, clock[reader])
        return at

    def run(at, work):
        while work > 1e-9:
            while at >= tick[0] + TICK:
                tick[:] = tick[0] + TICK, 0.0, tick[1] >= WARM
            slow = 1 if tick[2] else 2
            part = min(work, (tick[0] + TICK - at) / slow)
            tick[1] += part
            at += part * slow
            work -= part
        return at

    def place(item):
        pe, ring, reader, cost, deps = spec(item)
        clock["pe"] = run(clock["pe"], IDLE.get(item, 0) * 0.2135)
        at = start(item)
        order.append(item)
        if pe:
            clock["pe"] = at = run(at, pe)
            at += 0.2
        if reader and reader != "dma":
            at = clock[reader] = max(clock[reader], at) + cost
        elif reader:
            at += cost
        done[item] = at + 0.1
        if ring:
            banks[ring][count[ring] % len(banks[ring])] = at + 0.1
            count[ring] += 1

    streams = {"maxima": maxima, "scores": scores, "values": [("weights", "wvo")], "first": early[0],
               "second": early[1], "norms": norms, "tokens": tokens, "loads": loads, "hidden": hidden,
               "project": project, "maxima_T": [("maxT", c) for c in range(NC)], "sums": sums, "outs": outs}
    for item in opening:
        place(item)
    works = {name: sum(spec(x)[0] + spec(x)[3] for x in stream) for name, stream in streams.items()}
    left = dict(works)

    def late(name):
        ahead = left["scores"] / works["scores"] - left[name] / works[name]
        return PASSED[name] + (20.0 if name in LEADS and ahead > LEADS[name] else 0.0)

    while any(streams.values()):
        best = None
        for name, stream in streams.items():
            if stream and (at := start(stream[0])) is not None:
                at += late(name)
                if best is None or at < best[0]:
                    best = (at, name)
        assert best is not None
        item = streams[best[1]].pop(0)
        left[best[1]] -= spec(item)[0] + spec(item)[3]
        place(item)
    return order


ORDER = schedule()
VEC_UNITS = [x for x in ORDER if spec(x)[1] == "v"]
ACT_UNITS = [x for x in ORDER if spec(x)[1] == "a"]
VEC_AT = {x: n for n, x in enumerate(VEC_UNITS)}
ACT_AT = {x: n for n, x in enumerate(ACT_UNITS)}
SEL_AT = {x: n for n, x in enumerate(x for x in ORDER if x[0] == "sel")}


def build(nc, x, Wq, Wk, Wv, Wo, scale, fast_b, w_fc, w_proj, u, v, gate, consts, out):
    f32, bf16 = mybir.dt.float32, mybir.dt.bfloat16
    ALU, ACT, AX = mybir.AluOpType, mybir.ActivationFunctionType, mybir.AxisListType
    ctx = ExitStack()
    with ctx:
        def sb(name, shape, dt=f32):
            return ctx.enter_context(nc.sbuf_tensor(name, shape, dt))

        def ps(name, shape):
            return ctx.enter_context(nc.psum_tensor(name, shape, f32))

        def sem(name):
            return ctx.enter_context(nc.semaphore(name))

        x_sb = sb("x_sb", [P, NT, C])
        xn = sb("xn", [P, NT, C])
        xnT = sb("xnT", [P, B * T])
        k_sb = sb("k_sb", [P, CEND])
        ident = k_sb[:, CID:CID + P]
        ident16 = sb("ident16", [P, P], bf16)
        mask16 = sb("mask16", [P, P], bf16)
        mask_row = sb("mask_row", [P, CH])
        sel16 = sb("sel16", [P, 8, P], bf16)
        Wq_sb, Wk_sb = sb("Wq_sb", [NQ, C]), sb("Wk_sb", [NQ, C])
        Wv_sb, Wo_sb = sb("Wv_sb", [P, C]), sb("Wo_sb", [P, C])
        scale_c, gate_c = sb("scale_c", [NQ, 1]), sb("gate_c", [RANK, 1])
        mix = sb("mix", [NQ, NQ])
        wqkT = sb("wqkT", [P, 2 * NQ])
        wvoT = sb("wvoT", [P, 2, P])
        wfc_sb, wpj_sb = sb("wfc_sb", [P, HC, C]), sb("wpj_sb", [P, HID])
        u_sb, v_sb = sb("u_sb", [P, HC, RANK]), sb("v_sb", [RANK, C])
        fb_sb = sb("fb_sb", [RANK, RANK])
        loraB, uT = sb("loraB", [RANK, HID]), sb("uT", [RANK, HID])
        fc_sc, pj_sc = sb("fc_sc", [P, 3, HC]), sb("pj_sc", [P, 3])
        w1T, w2T = sb("w1T", [P, HID]), sb("w2T", [P, HC, C])
        stats, mv = sb("stats", [P, NT, 6]), sb("mv", [P, NT, 2])
        var, std, rstd, nwt = sb("var", [P, NT]), sb("std", [P, NT]), sb("rstd", [P, NT]), sb("nwt", [P, NT])
        Pr = sb("Pr", [P, PSLOTS, HG, CH])
        res = sb("res", [2 * NQ, 2, CH])
        part_hm, part_lo = sb("part_hm", [P, B * T], bf16), sb("part_lo", [2 * NQ, B * T], bf16)
        Qr, Kr = sb("Qr", [P, G, B * T], bf16), sb("Kr", [P, G, B * T], bf16)
        Kz = sb("Kz", [P, G, HG, T], bf16)
        V = sb("V", [P, NT, H, 32])
        r2 = sb("r2", [P, HC, B * T])
        pm = sb("pm", [P, 2, 2, TPC, HG])
        nmax, nres = sb("nmax", [P, 2, TPC, HG]), sb("nres", [P, TPC, HG])
        M16 = sb("M16", [P, 2, TPC, HG, 32], bf16)
        oT = sb("oT", [P, 2, CH])
        inv = sb("inv", [P, 2, TPC, HG])
        late = sb("late", [P, 2 * (TPC * C + CH)])
        on = late[:, 0:2 * TPC * C].rearrange("p (k n g h d) -> p k n g h d", k=2, n=TPC, g=G, h=HG)
        onT = late[:, 2 * TPC * C:].rearrange("p (k t) -> p k t", k=2)
        tern = late[:, :].rearrange("p (w s j c) -> p w s j c", w=2, s=2, j=HC)
        y_sb = xn

        vbank = [ps(f"vbank{i}", [P, CH]) for i in range(VB)]
        abank = [ps(f"abank{i}", [P, 2, CH]) for i in range(AB)]
        obank = ps("obank", [P, CH])

        ld_x = [sem(f"ld_x{i}") for i in range(4)]
        ld_id, ld_k, ld_qk, ld_vo, ld_fc, ld_pj, ld_lora = (
            sem(n) for n in ("ld_id", "ld_k", "ld_qk", "ld_vo", "ld_fc", "ld_pj", "ld_lora"))
        v_full, v_free, a_full, a_free = (sem(n) for n in ("v_full", "v_free", "a_full", "a_free"))
        kz_ready = [[sem(f"kz_ready{g}{n}") for n in range(NCH)] for g in range(G)]
        o_copied = sem("o_copied")
        dve_chain, pool_chain = sem("dve_chain"), sem("pool_chain")
        mix_ready, casts_ready, heads_zero, parts_zero, ones_ready, m_zero, mask_zero, keys_full, k_rows, keys_direct = (
            sem(n) for n in ("mix_ready", "casts_ready", "heads_zero", "parts_zero", "ones_ready", "m_zero", "mask_zero",
                                "keys_full", "k_rows", "keys_direct"))
        var_ready, std_ready, xn_ready = sem("var_ready"), sem("std_ready"), sem("xn_ready")
        hi_ready, mid_ready, lo_ready = sem("hi_ready"), sem("mid_ready"), sem("lo_ready")
        fc_signs, pj_signs, w1_ready, w2_ready = (sem(n) for n in ("fc_signs", "pj_signs", "w1_ready", "w2_ready"))
        r2_ready, maxima_ready, prep_ready, pv_done, stored = (
            sem(n) for n in ("r2_ready", "maxima_ready", "prep_ready", "pv_done", "stored"))

        last_full, last_summed = sem("last_full"), sem("last_summed")

        block = ctx.enter_context(nc.Block())

        @block.sync
        def _(sp):
            xv = x.rearrange("b (n p) c -> p (b n) c", p=P)
            ov = out.rearrange("b (n p) c -> p (b n) c", p=P)

            def load_tokens(q):
                sp.dma_start(x_sb[:, TPC * q:TPC * (q + 1), :], xv[:, TPC * q:TPC * (q + 1), :]).then_inc(ld_x[q], 16)

            load_tokens(0)
            sp.dma_start(k_sb[:, CID:CID + P], consts[:, CID:CID + P]).then_inc(ld_id, 16)
            sp.dma_start(k_sb[:, P:CEND], consts[:, P:CEND]).then_inc(ld_k, 16)
            sp.dma_start(wfc_sb[:, :, :], w_fc.rearrange("(j p) c -> p j c", p=P)).then_inc(ld_fc, 16)
            load_tokens(1)
            sp.dma_start(Wv_sb[:, :], Wv).then_inc(ld_vo, 16)
            sp.dma_start(Wo_sb[:, :], Wo).then_inc(ld_vo, 16)
            sp.dma_start(wpj_sb[:, :], w_proj).then_inc(ld_pj, 16)
            sp.dma_start(u_sb[:, :, :], u.rearrange("(j p) r -> p j r", p=P)).then_inc(ld_lora, 16)
            sp.dma_start(fb_sb[:, :], fast_b).then_inc(ld_lora, 16)
            sp.dma_start(v_sb[:, :], v).then_inc(ld_lora, 16)
            sp.dma_start(gate_c[:, :], gate.to_broadcast([RANK, 1])).then_inc(ld_lora, 16)
            load_tokens(2)
            load_tokens(3)
            sp.wait_ge(heads_zero, 1)
            for item in ORDER:
                if item[0] == "load":
                    _, k, chunk = item
                    b, g = k // G, k % G
                    sp.wait_ge(k_rows, SEL_AT[("sel", quarter(b, chunk), g)] + 1)
                    if k >= G:
                        c = (k - G) * NCH + NCH - 1
                        sp.wait_ge(a_full, ACT_AT[("st", c, len(steps(c)) - 1, 1)] + 1)
                    for h in range(HG):
                        r = slice(32 * h, 32 * h + 32)
                        sp.dma_start(Kz[r, g, h, chunk * CH:(chunk + 1) * CH],
                                     Kr[r, g, b * T + chunk * CH:b * T + (chunk + 1) * CH]
                                     ).then_inc(kz_ready[g][chunk], 16)
                elif item[0] == "y":
                    if item[1] != LAST:
                        sp.wait_ge(v_free, VEC_AT[item] + 1)
                    else:
                        sp.wait_ge(last_summed, item[2] + 1)
                    t0 = item[1] * TPC + item[2] * TPC // 2
                    sp.dma_start(ov[:, t0:t0 + TPC // 2, :], y_sb[:, t0:t0 + TPC // 2, :]).then_inc(stored, 16)
            sp.wait_ge(stored, 16 * B * NCH * 2)

        @block.gpsimd
        def _(pool):
            chain = [0]

            def link(ins):
                chain[0] += 1
                ins.then_inc(pool_chain, 1)
                pool.wait_ge(pool_chain, chain[0])

            nc.gpsimd.memset(part_hm[:, :].bitcast(f32), 0.0).then_inc(parts_zero, 1)
            nc.gpsimd.memset(Kz[:, :, :, :].rearrange("p g h t -> p (g h t)").bitcast(f32), 0.0).then_inc(heads_zero, 1)
            nc.gpsimd.memset(M16[:, :, :, :, :].rearrange("p s n h r -> p (s n h r)").bitcast(f32), 0.0
                             ).then_inc(m_zero, 1)
            pool.wait_ge(m_zero, 1)

            wp = wpj_sb[:, :].rearrange("p (j c) -> p j c", j=HC)
            ternaries = ((wfc_sb[:, :, :], fc_sc[:, 0, :, None].to_broadcast([P, HC, C]), fc_signs, w1_ready),
                         (wp, pj_sc[:, 0:1, None].to_broadcast([P, HC, C]), pj_signs, w2_ready))
            for item in ORDER:
                if item[0] == "ternary":
                    w, sc, signs, ready = ternaries[item[1]]
                    pool.wait_ge(signs, 2)
                    above, below = tern[:, item[1], 0, :, :], tern[:, item[1], 1, :, :]
                    link(nc.gpsimd.tensor_tensor(above, above, below, ALU.subtract))
                    link(nc.gpsimd.tensor_tensor(below, above, w, ALU.subtract))
                    link(nc.gpsimd.tensor_tensor(below, below, w, ALU.add))
                    nc.gpsimd.tensor_tensor(w, below, sc, ALU.mult).then_inc(ready, 1)
                elif item[0] == "square":
                    f = item[1]
                    q, j = f // FP, 2 * (f % FP)
                    r = r2[:, j:j + 2, q * CH:(q + 1) * CH]
                    pool.wait_ge(a_free, ACT_AT[("ffn", f)] + 1)
                    nc.gpsimd.tensor_tensor(r, r, r, ALU.mult).then_inc(r2_ready, 1)
                elif item[0] == "prep":
                    c = item[1]
                    s = c % 2
                    pool.wait_ge(maxima_ready, c + 1)
                    if c >= 2:
                        pool.wait_ge(v_full, VEC_AT[("maxT", c - 2)] + 1)
                    neg = nmax[:, s, :, :]
                    m = [M16[:, s, :, :, MROW + k] for k in range(NPART)]
                    link(nc.gpsimd.tensor_copy(m[0], neg))
                    link(nc.gpsimd.tensor_tensor(nres[:, :, :], neg, m[0], ALU.subtract))
                    link(nc.gpsimd.tensor_copy(m[1], nres[:, :, :]))
                    nc.gpsimd.tensor_tensor(m[2], nres[:, :, :], m[1], ALU.subtract).then_inc(prep_ready, 1)
                    pool.wait_ge(prep_ready, c + 1)

        @block.vector
        def _(dve):
            chain = [0]

            def link(ins):
                chain[0] += 1
                ins.then_inc(dve_chain, 1)
                dve.wait_ge(dve_chain, chain[0])

            def filled(unit):
                dve.wait_ge(v_full, VEC_AT[unit] + 1)
                return vbank[VEC_AT[unit] % VB]

            nc.vector.memset(mask_row[:, :], 0.0).then_inc(mask_zero, 1)
            nc.vector.memset(V[:, :, :, HD:32], 1.0).then_inc(ones_ready, 1)
            dve.wait_ge(mask_zero, 1)
            for item in ORDER:
                kind = item[0]
                if kind == "var":
                    q = item[1]
                    dve.wait_ge(ld_x[q], 16)
                    for n in range(TPC * q, TPC * (q + 1)):
                        last = nc.vector.bn_stats(stats[:, n, :], x_sb[:, n, :])
                    link(last)
                    for n in range(TPC * q, TPC * (q + 1)):
                        last = nc.vector.bn_aggr(mv[:, n, :], stats[:, n, :])
                    link(last)
                    s = slice(TPC * q, TPC * (q + 1))
                    nc.vector.tensor_scalar(var[:, s], mv[:, s, 1], LN_EPS, None, ALU.add).then_inc(var_ready, 1)
                elif kind == "mix":
                    dve.wait_ge(ld_qk, 48)
                    dve.wait_ge(ld_id, 16)
                    dve.wait_ge(ld_k, 16)
                    nc.vector.scalar_tensor_tensor(out=mix[:, :], in0=k_sb[0:NQ, CID:CID + NQ],
                                                   scalar=scale_c[:, 0:1], in1=k_sb[0:NQ, CDIR:CDIR + NQ],
                                                   op0=ALU.mult, op1=ALU.add).then_inc(mix_ready, 1)
                elif kind == "xn":
                    q = item[1]
                    s = slice(TPC * q, TPC * (q + 1))
                    dve.wait_ge(std_ready, q + 1)
                    link(nc.vector.reciprocal(rstd[:, s], std[:, s]))
                    link(nc.vector.tensor_tensor(nwt[:, s], rstd[:, s], rstd[:, s], ALU.mult))
                    link(nc.vector.tensor_tensor(nwt[:, s], nwt[:, s], var[:, s], ALU.mult))
                    link(nc.vector.tensor_scalar(nwt[:, s], nwt[:, s], -0.5, 1.5, ALU.mult, ALU.add))
                    link(nc.vector.tensor_tensor(rstd[:, s], rstd[:, s], nwt[:, s], ALU.mult))
                    for n in range(TPC * q, TPC * (q + 1)):
                        last = nc.vector.tensor_scalar(xn[:, n, :], x_sb[:, n, :], mv[:, n, 0:1], rstd[:, n:n + 1],
                                                       ALU.subtract, ALU.mult)
                    last.then_inc(xn_ready, 1)
                elif kind == "casts":
                    dve.wait_ge(ld_id, 16)
                    dve.wait_ge(ld_k, 16)
                    for dst, src in ((ident16[:, :], k_sb[:, CID:CID + P]), (mask16[:, :], k_sb[:, CMASK:CMASK + P]),
                                     (sel16[:, :, :], k_sb[:, CSEL:CDIR].rearrange("p (s c) -> p s c", c=P))):
                        nc.vector.tensor_copy(dst, src).then_inc(casts_ready, 1)
                    link(nc.vector.tensor_copy(mask_row[:, CH - P:CH], k_sb[:, CMASK:CMASK + P]))
                elif kind == "weights":
                    src = filled(item)
                    if item[1] == "wqk":
                        ins = nc.vector.tensor_copy(wqkT[:, :], src[:, 0:2 * NQ])
                    elif item[1] == "wvo":
                        ins = nc.vector.tensor_copy(wvoT[:, :, :], src[:, 0:2 * P].rearrange("p (k c) -> p k c", c=P))
                    elif item[1] == "lora_u":
                        ins = nc.vector.tensor_copy(uT[:, :], src[0:RANK, :])
                    elif item[1] == "lora_b":
                        ins = nc.vector.tensor_scalar(loraB[:, :], src[0:RANK, :], gate_c[:, 0:1], None, ALU.mult)
                    elif item[1] == "w1":
                        ins = nc.vector.tensor_copy(w1T[:, :], src[:, :])
                    else:
                        ins = nc.vector.tensor_copy(w2T[:, :, :], src[:, :].rearrange("p (j c) -> p j c", j=HC))
                    ins.then_inc(v_free, 1)
                elif kind == "qk":
                    q = item[1]
                    cols = slice(q * CH, (q + 1) * CH)
                    src = filled(item)
                    dve.wait_ge(hi_ready, q + 1)
                    if q >= 2:
                        dve.wait_ge(mid_ready, q - 1)
                        dve.wait_ge(lo_ready, q - 1)
                    nc.vector.tensor_tensor(res[:, q % 2, :], src[0:2 * NQ, :], part_hm[0:2 * NQ, cols],
                                            ALU.subtract).then_inc(v_free, 1)
                elif kind == "low":
                    q = item[1]
                    cols = slice(q * CH, (q + 1) * CH)
                    dve.wait_ge(mid_ready, q + 1)
                    nc.vector.tensor_tensor(part_lo[:, cols], res[:, q % 2, :], part_hm[64:64 + 2 * NQ, cols],
                                            ALU.subtract).then_inc(lo_ready, 1)
                    dve.wait_ge(lo_ready, q + 1)
                elif kind == "direct":
                    dve.wait_ge(keys_full, 1)
                    dve.wait_ge(heads_zero, 1)
                    for h in range(HG // 2, HG):
                        r = slice(32 * h, 32 * h + 32)
                        last = nc.vector.tensor_scalar(Kz[r, 0, h, 0:CH], abank[ACT_AT[("sel", 0, 0)] % AB][r, 1, :],
                                                       k_sb[r, CONE:CONE + 1], None, ALU.add)
                    last.then_inc(keys_direct, 1)
                elif kind == "signs":
                    if item[1] == 0:
                        dve.wait_ge(ld_fc, 16)
                        link(nc.vector.tensor_reduce(out=fc_sc[:, 1, :], in_=wfc_sb[:, :, :], op=ALU.add, axis=AX.X,
                                                     apply_absolute_value=True))
                        link(nc.vector.tensor_scalar(fc_sc[:, 0, :], fc_sc[:, 1, :], 1.0 / C, MIN_SCALE,
                                                     ALU.mult, ALU.max))
                        nc.vector.tensor_scalar(fc_sc[:, 1, :], fc_sc[:, 0, :], 0.5, None, ALU.mult)
                        link(nc.vector.tensor_scalar(fc_sc[:, 2, :], fc_sc[:, 0, :], -0.5, None, ALU.mult))
                        for k, op in enumerate((ALU.is_gt, ALU.is_lt)):
                            nc.vector.tensor_tensor(tern[:, 0, k, :, :], wfc_sb[:, :, :],
                                                    fc_sc[:, 1 + k, :, None].to_broadcast([P, HC, C]),
                                                    op).then_inc(fc_signs, 1)
                    else:
                        dve.wait_ge(ld_pj, 16)
                        link(nc.vector.tensor_reduce(out=pj_sc[:, 1:2], in_=wpj_sb[:, :], op=ALU.add, axis=AX.X,
                                                     apply_absolute_value=True))
                        link(nc.vector.tensor_scalar(pj_sc[:, 0:1], pj_sc[:, 1:2], 1.0 / HID, MIN_SCALE,
                                                     ALU.mult, ALU.max))
                        nc.vector.tensor_scalar(pj_sc[:, 1:2], pj_sc[:, 0:1], 0.5, None, ALU.mult)
                        link(nc.vector.tensor_scalar(pj_sc[:, 2:3], pj_sc[:, 0:1], -0.5, None, ALU.mult))
                        for k, op in enumerate((ALU.is_gt, ALU.is_lt)):
                            nc.vector.tensor_scalar(tern[:, 1, k, :, :].rearrange("p j c -> p (j c)"), wpj_sb[:, :],
                                                    pj_sc[:, 1 + k:2 + k], None, op).then_inc(pj_signs, 1)
                elif kind == "max":
                    c = item[1]
                    i, half, h0, heads, keys = max_units(c)[item[2]]
                    if item[2] == 0 and c >= 2:
                        dve.wait_ge(prep_ready, c - 1)
                    src = filled(item)
                    if half < coords(c)[2]:
                        last = nc.vector.tensor_reduce(out=pm[:, c % 2, half, i % TPC, h0:h0 + 1], in_=src[:, 0:keys],
                                                       op=ALU.max, axis=AX.X, negate=True)
                    else:
                        for n in range(heads):
                            s_n = src[:, n * keys:(n + 1) * keys]
                            last = nc.vector.tensor_tensor_reduce(
                                out=s_n, in0=s_n,
                                in1=mask_row[:, CH - keys:CH], scale=1.0, scalar=NEG, op0=ALU.add, op1=ALU.max,
                                accum_out=pm[:, c % 2, half, i % TPC, h0 + n:h0 + n + 1])
                    last.then_inc(v_free, 1)
                elif kind == "top":
                    c = item[1]
                    dve.wait_ge(v_free, VEC_AT[("max", c, len(max_units(c)) - 1)] + 1)
                    if coords(c)[2]:
                        ins = nc.vector.scalar_tensor_tensor(out=nmax[:, c % 2, :, :], in0=pm[:, c % 2, 1, :, :],
                                                             scalar=-1.0, in1=pm[:, c % 2, 0, :, :],
                                                             op0=ALU.mult, op1=ALU.min)
                    else:
                        ins = nc.vector.tensor_scalar(nmax[:, c % 2, :, :], pm[:, c % 2, 0, :, :], -1.0, None, ALU.mult)
                    ins.then_inc(maxima_ready, 1)
                elif kind == "maxT":
                    b, g, chunk = coords(item[1])
                    q = Qr[:, g, b * T + chunk * CH:b * T + (chunk + 1) * CH]
                    src = filled(item)
                    nc.vector.tensor_tensor(q, src[:, :], q, ALU.add).then_inc(v_free, 1)
                elif kind == "oT":
                    c = item[1]
                    b, g, chunk = coords(c)
                    o = filled(item)[:, :].rearrange("p (n h r) -> p n h r", n=TPC, h=HG)
                    link(nc.vector.reciprocal(inv[:, c % 2, :, :], o[:, :, :, HD]))
                    if b and g == 0:
                        dve.wait_ge(v_full, VEC_AT[("oB", quarter(b - 1, chunk))] + 1)
                    nc.vector.tensor_tensor(on[:, chunk, :, g, :, :], o[:, :, :, 0:HD],
                                            inv[:, c % 2, :, :, None].to_broadcast([P, TPC, HG, HD]),
                                            ALU.mult).then_inc(v_free, 1)
                elif kind == "oB":
                    src = filled(item)
                    nc.vector.tensor_copy(onT[:, item[1] % NCH, :], src[:, :]).then_inc(v_free, 1)
                elif kind == "y":
                    _, q, half = item
                    t0, n = q * TPC + half * TPC // 2, TPC // 2
                    if q != LAST:
                        src, done = filled(item)[:, 0:n * P], v_free
                    else:
                        dve.wait_ge(last_full, half + 1)
                        src, done = abank[ACT_AT[("y0", LAST, 0)] % AB][:, half, 0:n * P], last_summed
                    nc.vector.tensor_tensor(y_sb[:, t0:t0 + n, :], src.rearrange("p (n c) -> p n c", n=n),
                                            x_sb[:, t0:t0 + n, :], ALU.add).then_inc(done, 1)

        @block.scalar
        def _(act):
            def filled(unit):
                act.wait_ge(a_full, ACT_AT[unit] + 1)
                return abank[ACT_AT[unit] % AB]

            act.dma_start(Wq_sb[:, :], Wq).then_inc(ld_qk, 16)
            act.dma_start(Wk_sb[:, :], Wk).then_inc(ld_qk, 16)
            act.dma_start(scale_c[:, :], scale.to_broadcast([NQ, 1])).then_inc(ld_qk, 16)
            for item in ORDER:
                kind = item[0]
                if kind == "std":
                    s = slice(TPC * item[1], TPC * (item[1] + 1))
                    act.wait_ge(var_ready, item[1] + 1)
                    nc.scalar.activation(std[:, s], var[:, s], ACT.Sqrt).then_inc(std_ready, 1)
                elif kind == "xT":
                    src = filled(item)
                    nc.scalar.copy(xnT[:, item[1] * CH:(item[1] + 1) * CH], src[:, 0, :]).then_inc(a_free, 1)
                elif kind == "qk":
                    q = item[1]
                    act.wait_ge(v_full, VEC_AT[item] + 1)
                    if q == 0:
                        act.wait_ge(parts_zero, 1)
                    nc.scalar.copy(part_hm[0:2 * NQ, q * CH:(q + 1) * CH],
                                   vbank[VEC_AT[item] % VB][0:2 * NQ, :]).then_inc(hi_ready, 1)
                elif kind == "mid":
                    q = item[1]
                    cols = slice(q * CH, (q + 1) * CH)
                    act.wait_ge(v_free, VEC_AT[("qk", q)] + 1)
                    nc.scalar.copy(part_hm[64:64 + 2 * NQ, cols], res[:, q % 2, :]).then_inc(mid_ready, 1)
                elif kind == "sel":
                    _, q, g = item
                    cols = slice(q * CH, (q + 1) * CH)
                    act.wait_ge(keys_full, SEL_AT[item] + 1)
                    keys = abank[ACT_AT[item] % AB][:, 1, :]
                    if q + g:
                        nc.scalar.activation(Kr[:, g, cols], keys, ACT.Identity,
                                             bias=k_sb[:, CONE:CONE + 1]).then_inc(k_rows, 1)
                    else:
                        act.wait_ge(heads_zero, 1)
                        for h in range(HG // 2):
                            r = slice(32 * h, 32 * h + 32)
                            last = nc.scalar.activation(Kz[r, g, h, cols], keys[r, :], ACT.Identity,
                                                        bias=k_sb[r, CONE:CONE + 1])
                        last.then_inc(k_rows, 1)
                        act.wait_ge(keys_direct, 1)
                    nc.scalar.copy(Qr[:, g, cols], filled(item)[:, 0, :]).then_inc(a_free, 1)
                elif kind == "v":
                    q = item[1]
                    src = filled(item)
                    if q == 0:
                        act.wait_ge(ones_ready, 1)
                    nc.scalar.copy(V[:, q * TPC:(q + 1) * TPC, :, 0:HD],
                                   src[:, 0, :].rearrange("p (n h d) -> p n h d", h=H, d=HD)).then_inc(a_free, 1)
                elif kind == "ffn":
                    q, j = item[1] // FP, 2 * (item[1] % FP)
                    src = filled(item)
                    nc.scalar.activation(r2[:, j:j + 2, q * CH:(q + 1) * CH], src[:, :, :],
                                         ACT.Relu).then_inc(a_free, 1)
                elif kind == "st":
                    _, c, step, pair = item
                    n = STEP0[c] + step
                    cols = steps(c)[step][2]
                    if n >= PSLOTS and pair == 0:
                        act.wait_ge(pv_done, n - PSLOTS + 1)
                    src = filled(item)
                    nc.scalar.activation(Pr[:, n % PSLOTS, 2 * pair:2 * pair + 2, 0:cols], src[:, :, 0:cols],
                                         ACT.Exp).then_inc(a_free, 1)
                elif kind == "ocopy":
                    c = item[1]
                    act.wait_ge(pv_done, STEP0[c + 1])
                    if c >= 2:
                        act.wait_ge(v_full, VEC_AT[("oT", c - 2)] + 1)
                    nc.scalar.copy(oT[:, c % 2, :], obank[:, :]).then_inc(o_copied, 1)

        @block.tensor
        def _(pe):
            def empty(unit):
                if unit in VEC_AT:
                    n = VEC_AT[unit]
                    if n >= VB:
                        pe.wait_ge(v_free, n - VB + 1)
                    return vbank[n % VB]
                n = ACT_AT[unit]
                if n >= AB:
                    pe.wait_ge(a_free, n - AB + 1)
                return abank[n % AB]

            def vec_read(unit):
                pe.wait_ge(v_free, VEC_AT[unit] + 1)

            def act_read(unit):
                pe.wait_ge(a_free, ACT_AT[unit] + 1)

            def hidden_part(o, q, n, first):
                t = (q * TPC + n) * P
                at = n % 2 * P
                for j in range(HC):
                    nc.tensor.matmul(o[:, at:at + P], r2[:, j, t:t + P], w2T[:, j, :],
                                     start=j == 0 and first, stop=False)

            def keep_clock(n):
                zeros = mask_row[:, 0:CH // 2].bitcast(bf16)
                for _ in range(n):
                    nc.tensor.matmul(obank[:, :], zeros[:, 0:P], zeros, start=True, stop=True)

            pe.wait_ge(mask_zero, 1)
            for item in ORDER:
                kind = item[0]
                if item in IDLE:
                    keep_clock(IDLE[item])
                if kind == "weights":
                    o = empty(item)
                    if item[1] == "wqk":
                        pe.wait_ge(ld_id, 16)
                        pe.wait_ge(ld_qk, 48)
                        pe.wait_ge(mix_ready, 1)
                        nc.tensor.matmul(o[:, 0:NQ], Wq_sb[:, :], mix[:, :], start=True, stop=True)
                        last = nc.tensor.matmul(o[:, NQ:2 * NQ], Wk_sb[:, :], k_sb[0:NQ, CID:CID + NQ],
                                                start=True, stop=True)
                    elif item[1] == "wvo":
                        pe.wait_ge(ld_vo, 32)
                        nc.tensor.transpose(o[:, 0:P], Wv_sb[:, :], ident)
                        last = nc.tensor.transpose(o[:, P:2 * P], Wo_sb[:, :], ident)
                    elif item[1] == "lora_u":
                        pe.wait_ge(ld_lora, 64)
                        for j in range(HC):
                            last = nc.tensor.transpose(o[0:RANK, j * P:(j + 1) * P], u_sb[:, j, :], ident)
                    elif item[1] == "lora_b":
                        vec_read(("weights", "lora_u"))
                        last = nc.tensor.matmul(o[0:RANK, :], fb_sb[:, :], uT[:, :], start=True, stop=True)
                    elif item[1] == "w1":
                        pe.wait_ge(w1_ready, 1)
                        vec_read(("weights", "lora_b"))
                        for j in range(HC):
                            nc.tensor.matmul(o[:, j * P:(j + 1) * P], wfc_sb[:, j, :], ident, start=True, stop=False)
                            last = nc.tensor.matmul(o[:, j * P:(j + 1) * P], v_sb[:, :], loraB[:, j * P:(j + 1) * P],
                                                    start=False, stop=True)
                    else:
                        pe.wait_ge(w2_ready, 1)
                        for j in range(HC):
                            last = nc.tensor.transpose(o[:, j * P:(j + 1) * P], wpj_sb[:, j * P:(j + 1) * P], ident)
                    last.then_inc(v_full, 1)
                elif kind == "xT":
                    q = item[1]
                    o = empty(item)
                    pe.wait_ge(xn_ready, q + 1)
                    if q == 0:
                        pe.wait_ge(ld_id, 16)
                    for n in range(TPC):
                        last = nc.tensor.transpose(o[:, 0, n * P:(n + 1) * P], xn[:, q * TPC + n, :], ident)
                    last.then_inc(a_full, 1)
                elif kind == "qk":
                    q = item[1]
                    o = empty(item)
                    act_read(("xT", q))
                    vec_read(("weights", "wqk"))
                    nc.tensor.matmul(o[0:2 * NQ, :], wqkT[:, :], xnT[:, q * CH:(q + 1) * CH], start=True,
                                     stop=True).then_inc(v_full, 1)
                elif kind == "sel":
                    _, q, g = item
                    cols = slice(q * CH, (q + 1) * CH)
                    o = empty(item)
                    pe.wait_ge(casts_ready, 3)
                    pe.wait_ge(mid_ready, q + 1)
                    pe.wait_ge(lo_ready, q + 1)
                    for side in (1, 0):
                        nc.tensor.matmul(o[:, side, :], sel16[:, 2 * side * G + g, :], part_hm[:, cols],
                                         start=True, stop=False)
                        last = nc.tensor.matmul(o[:, side, :], sel16[0:2 * NQ, (2 * side + 1) * G + g, :],
                                                part_lo[:, cols], start=False, stop=True)
                        last.then_inc(keys_full if side else a_full, 1)
                elif kind == "v":
                    q = item[1]
                    o = empty(item)
                    act_read(("xT", q))
                    vec_read(("weights", "wvo"))
                    for n in range(TPC):
                        t = slice((q * TPC + n) * P, (q * TPC + n + 1) * P)
                        last = nc.tensor.matmul(o[:, 0, n * P:(n + 1) * P], xnT[:, t], wvoT[:, 0, :],
                                                start=True, stop=True)
                    last.then_inc(a_full, 1)
                elif kind == "ffn":
                    q, j = item[1] // FP, 2 * (item[1] % FP)
                    o = empty(item)
                    vec_read(("weights", "w1"))
                    act_read(("xT", q))
                    for k in range(2):
                        last = nc.tensor.matmul(o[:, k, :], w1T[:, (j + k) * P:(j + k + 1) * P],
                                                xnT[:, q * CH:(q + 1) * CH], start=True, stop=True)
                    last.then_inc(a_full, 1)
                elif kind == "max":
                    c = item[1]
                    b, g, chunk = coords(c)
                    i, half, h0, heads, keys = max_units(c)[item[2]]
                    if item[2] == 0:
                        act_read(("sel", quarter(b, chunk), g))
                        if c == 0:
                            pe.wait_ge(keys_direct, 1)
                        else:
                            pe.wait_ge(kz_ready[g][chunk], 16 * HG * (b + (g > 0 or chunk > 0)))
                    o = empty(item)
                    q0 = b * T + i * P
                    for n in range(heads):
                        last = nc.tensor.matmul(o[:, n * keys:(n + 1) * keys],
                                                Qr[:, g, q0:q0 + P], Kz[:, g, h0 + n, half * CH:half * CH + keys],
                                                start=True, stop=True)
                    last.then_inc(v_full, 1)
                elif kind == "maxT":
                    c = item[1]
                    o = empty(item)
                    pe.wait_ge(prep_ready, c + 1)
                    for n in range(TPC):
                        last = nc.tensor.matmul(o[:, n * P:(n + 1) * P],
                                                M16[:, c % 2, n, :, :].rearrange("p j r -> p (j r)"), ident16[:, :],
                                                start=True, stop=True)
                    last.then_inc(v_full, 1)
                elif kind == "st":
                    _, c, step, pair = item
                    b, g, chunk = coords(c)
                    j, first, cols = steps(c)[step]
                    o = empty(item)
                    if step == 0 and pair == 0:
                        vec_read(("maxT", c))
                    q0 = b * T + chunk * CH + first
                    for n in range(2):
                        diag = j >= TPC * chunk
                        last = nc.tensor.matmul(o[:, n, 0:cols], Kz[:, g, 2 * pair + n, j * P:(j + 1) * P],
                                                Qr[:, g, q0:q0 + cols], start=True, stop=not diag)
                        if diag:
                            last = nc.tensor.matmul(o[:, n, 0:P], mask16[:, :], ident16[:, :],
                                                    start=False, stop=True)
                    last.then_inc(a_full, 1)
                elif kind == "pv":
                    _, c, step = item
                    b, g, chunk = coords(c)
                    j, first, cols = steps(c)[step]
                    n = STEP0[c] + step
                    if step == 0:
                        act_read(("v", quarter(b, chunk)))
                        if c:
                            pe.wait_ge(o_copied, c)
                    act_read(("st", c, step, 1))
                    for h in range(HG):
                        last = nc.tensor.matmul(obank[32 * h:32 * h + 32, first:CH],
                                                V[:, b * TPB + j, HG * g + h, :], Pr[:, n % PSLOTS, h, 0:cols],
                                                start=step == 0, stop=step == len(steps(c)) - 1)
                    last.then_inc(pv_done, 1)
                elif kind == "oT":
                    c = item[1]
                    o = empty(item)
                    pe.wait_ge(o_copied, c + 1)
                    for n in range(TPC):
                        last = nc.tensor.transpose(o[:, n * P:(n + 1) * P], oT[:, c % 2, n * P:(n + 1) * P], ident)
                    last.then_inc(v_full, 1)
                elif kind == "oB":
                    b, chunk = item[1] // NCH, item[1] % NCH
                    o = empty(item)
                    vec_read(("oT", (b * G + G - 1) * NCH + chunk))
                    for n in range(TPC):
                        last = nc.tensor.transpose(o[:, n * P:(n + 1) * P],
                                                   on[:, chunk, n, :, :, :].rearrange("p g h d -> p (g h d)"), ident)
                    last.then_inc(v_full, 1)
                elif kind == "y0":
                    _, q, n = item
                    if n == 0:
                        last_pair = empty(item)
                        vec_read(("weights", "w2"))
                        pe.wait_ge(r2_ready, (q + 1) * FP)
                    hidden_part(last_pair[:, n // 2, :], q, n, first=n % 2 == 0)
                elif kind == "y":
                    _, q, half = item
                    o = last_pair[:, half, :] if q == LAST else empty(item)
                    vec_read(("oB", q))
                    vec_read(("weights", "w2"))
                    pe.wait_ge(r2_ready, (q + 1) * FP)
                    for n in range(2 * half, 2 * half + 2):
                        if q != LAST:
                            hidden_part(o, q, n, first=True)
                        at = n % 2 * P
                        last = nc.tensor.matmul(o[:, at:at + P], onT[:, q % NCH, n * P:(n + 1) * P],
                                                wvoT[:, 1, :], start=False, stop=q != LAST or n % 2 == 1)
                    last.then_inc(last_full if q == LAST else v_full, 1)


_INS = ["L0_attn_x", "L0_attn_Wq", "L0_attn_Wk", "L0_attn_Wv", "L0_attn_Wo", "L0_attn_scale", "L0_ffn_fast_b",
        "L0_ffn_w_fc", "L0_ffn_w_proj", "L0_ffn_u", "L0_ffn_v", "L0_ffn_gate"]


def kernel(**inputs):
    import numpy as _np
    import concourse.bacc as _bacc
    from concourse import mybir as _mybir
    from concourse.bass_utils import run_bass_kernel_spmd as _run

    nc = _bacc.Bacc("TRN2", target_bir_lowering=False, num_devices=1)
    arrays, args = {}, []
    for name in _INS:
        a = _np.ascontiguousarray(inputs[name])
        if a.ndim == 0:
            a = a.reshape(1, 1)
        arrays[f"in_{name}"] = a
        args.append(nc.dram_tensor(f"in_{name}", a.shape, _mybir.dt.from_np(a.dtype), kind="ExternalInput").ap())
    k = constants()
    arrays["in_consts"] = k
    args.append(nc.dram_tensor("in_consts", k.shape, _mybir.dt.float32, kind="ExternalInput").ap())
    args.append(nc.dram_tensor("out_y", (B, T, C), _mybir.dt.float32, kind="ExternalOutput").ap())
    build(nc, *args)
    r = _run(nc, [arrays], core_ids=[0])
    return r.results[0]["out_y"]
```
